# Optimizing a Trainium2 kernel written in Bass

```python
import numpy as np
import jax
import jax.numpy as jnp

def _softmax(x, axis=-1):
    return jax.nn.softmax(x, axis=axis)

def _gelu(x):
    return jax.nn.gelu(x, approximate=True)

def _silu(x):
    return jax.nn.silu(x)

def _sigmoid(x):
    return jax.nn.sigmoid(x)

def _layernorm(x, axis=-1, eps=1e-05):
    m = jnp.mean(x, axis=axis, keepdims=True)
    v = jnp.var(x, axis=axis, keepdims=True)
    return (x - m) / jnp.sqrt(v + eps)

def _scatter_add(tgt, idx, src, axis=0):
    return tgt.at[idx].add(src)

def _segment_sum(src, seg, n):
    return jax.ops.segment_sum(src, seg, n)
kernel_name = 'mk_prb_d1_jaxref_r4_21e582'

def setup_inputs(seed: int=0):
    np.random.seed(seed)
    _w = jnp.asarray

    def _L0_attn_setup():
        import jax, jax.numpy as jnp
        import numpy as np
        B, N, D, H = (4, 512, 256, 16)
        Dh = D // H
        ROPE_THETA = 10000.0

        def _rope(x):
            n, d = (x.shape[-2], x.shape[-1])
            inv_freq = 1.0 / ROPE_THETA ** (jnp.arange(0, d, 2, dtype=jnp.float32) / d)
            freqs = jnp.arange(n, dtype=jnp.float32)[:, None] * inv_freq[None, :]
            freqs = jnp.repeat(freqs, 2, axis=-1)
            cos, sin = (jnp.cos(freqs), jnp.sin(freqs))
            x1 = x[..., ::2]
            x2 = x[..., 1::2]
            rot = jnp.stack([-x2, x1], axis=-1).reshape(x.shape)
            return x * cos + rot * sin
        key = jax.random.key(seed)
        ks = jax.random.split(key, 9)
        s = 0.02
        return {'x': jax.random.normal(ks[0], (B, N, D), dtype=jnp.float32), 'Wq': jax.random.normal(ks[1], (D, D), dtype=jnp.float32) * s, 'bq': jax.random.normal(ks[2], (D,), dtype=jnp.float32) * s, 'Wk': jax.random.normal(ks[3], (D, D), dtype=jnp.float32) * s, 'bk': jax.random.normal(ks[4], (D,), dtype=jnp.float32) * s, 'Wv': jax.random.normal(ks[5], (D, D), dtype=jnp.float32) * s, 'bv': jax.random.normal(ks[6], (D,), dtype=jnp.float32) * s, 'Wo': jax.random.normal(ks[7], (D, D), dtype=jnp.float32) * s, 'bo': jax.random.normal(ks[8], (D,), dtype=jnp.float32) * s}
    _L0_attn_in = _L0_attn_setup()

    def _L0_ffn_setup():
        import jax, jax.numpy as jnp
        import numpy as np
        from math import ceil
        CAPACITY_FACTOR = 2.0
        MIN_CAPACITY = 4
        key = jax.random.key(seed)
        ks = jax.random.split(key, 4)
        B, S, D, Di, E = (4, 512, 256, 1024, 8)
        x = jax.random.normal(ks[0], (B, S, D), dtype=jnp.float32)
        Wr = jax.random.normal(ks[1], (D, E), dtype=jnp.float32) * D ** (-0.5)
        W1 = jax.random.normal(ks[2], (E, D, Di), dtype=jnp.float32) * D ** (-0.5)
        b1 = jnp.zeros((E, Di), dtype=jnp.float32)
        W2 = jax.random.normal(ks[3], (E, Di, D), dtype=jnp.float32) * Di ** (-0.5)
        b2 = jnp.zeros((E, D), dtype=jnp.float32)
        return {'x': x, 'Wr': Wr, 'W1': W1, 'b1': b1, 'W2': W2, 'b2': b2}
    _L0_ffn_in = _L0_ffn_setup()
    _d = {'L0_attn_x': _L0_attn_in['x'], 'L0_attn_Wq': _L0_attn_in['Wq'], 'L0_attn_bq': _L0_attn_in['bq'], 'L0_attn_Wk': _L0_attn_in['Wk'], 'L0_attn_bk': _L0_attn_in['bk'], 'L0_attn_Wv': _L0_attn_in['Wv'], 'L0_attn_bv': _L0_attn_in['bv'], 'L0_attn_Wo': _L0_attn_in['Wo'], 'L0_attn_bo': _L0_attn_in['bo'], 'L0_ffn_Wr': _L0_ffn_in['Wr'], 'L0_ffn_W1': _L0_ffn_in['W1'], 'L0_ffn_b1': _L0_ffn_in['b1'], 'L0_ffn_W2': _L0_ffn_in['W2'], 'L0_ffn_b2': _L0_ffn_in['b2']}
    _x0 = _d['L0_attn_x']
    _d['L0_attn_x'] = jax.random.normal(jax.random.fold_in(jax.random.key(seed), 1), (4, 1024, 256), dtype=_x0.dtype)
    del _x0
    return _d

def reference(L0_attn_x, L0_attn_Wq, L0_attn_bq, L0_attn_Wk, L0_attn_bk, L0_attn_Wv, L0_attn_bv, L0_attn_Wo, L0_attn_bo, L0_ffn_Wr, L0_ffn_W1, L0_ffn_b1, L0_ffn_W2, L0_ffn_b2):

    def _L0_attn_ref(x, Wq, bq, Wk, bk, Wv, bv, Wo, bo):
        import jax, jax.numpy as jnp
        import numpy as np
        B, N, D, H = (4, 512, 256, 16)
        Dh = D // H
        ROPE_THETA = 10000.0

        def _rope(x):
            n, d = (x.shape[-2], x.shape[-1])
            inv_freq = 1.0 / ROPE_THETA ** (jnp.arange(0, d, 2, dtype=jnp.float32) / d)
            freqs = jnp.arange(n, dtype=jnp.float32)[:, None] * inv_freq[None, :]
            freqs = jnp.repeat(freqs, 2, axis=-1)
            cos, sin = (jnp.cos(freqs), jnp.sin(freqs))
            x1 = x[..., ::2]
            x2 = x[..., 1::2]
            rot = jnp.stack([-x2, x1], axis=-1).reshape(x.shape)
            return x * cos + rot * sin
        b, n, d = x.shape
        split = lambda t: t.reshape(b, n, H, Dh).transpose(0, 2, 1, 3)
        q = split(x @ Wq + bq)
        k = split(x @ Wk + bk)
        v = split(x @ Wv + bv)
        q = _rope(q)
        k = _rope(k)
        scores = jnp.einsum('bhnd,bhmd->bhnm', q, k) / jnp.sqrt(jnp.float32(d))
        weights = jax.nn.softmax(scores, axis=-1)
        inter = jnp.einsum('bhnm,bhmd->bhnd', weights, v)
        inter = inter.transpose(0, 2, 1, 3).reshape(b, n, d)
        return inter @ Wo + bo

    def _L0_ffn_ref(x, Wr, W1, b1, W2, b2):
        import jax, jax.numpy as jnp
        import numpy as np
        from math import ceil
        CAPACITY_FACTOR = 2.0
        MIN_CAPACITY = 4
        B, S, D = x.shape
        E = Wr.shape[1]
        N = B * S
        k = max(MIN_CAPACITY, ceil(N * CAPACITY_FACTOR / E))
        xt = x.reshape(N, D)
        scores = jax.nn.softmax(xt @ Wr, axis=-1)
        G, idx = jax.lax.top_k(scores.T, k)
        X_in = xt[idx]
        h = jax.nn.gelu(jnp.einsum('ekd,edh->ekh', X_in, W1) + b1[:, None, :], approximate=False)
        X_e = jnp.einsum('ekh,ehd->ekd', h, W2) + b2[:, None, :]
        contrib = (G[..., None] * X_e).reshape(E * k, D)
        out = jnp.zeros((N, D), dtype=x.dtype).at[idx.reshape(-1)].add(contrib)
        return out.reshape(B, S, D)
    x = L0_attn_x
    xn = _layernorm(x, axis=-1)
    x = x + _L0_attn_ref(xn, L0_attn_Wq, L0_attn_bq, L0_attn_Wk, L0_attn_bk, L0_attn_Wv, L0_attn_bv, L0_attn_Wo, L0_attn_bo) + _L0_ffn_ref(xn, L0_ffn_Wr, L0_ffn_W1, L0_ffn_b1, L0_ffn_W2, L0_ffn_b2)
    return x

_drawn_inputs = setup_inputs


def setup_inputs(seed=0):
    import zlib

    import numpy as np

    out = dict(_drawn_inputs(seed))
    spreads = {'L0_ffn_b1': (0.0, 0.267), 'L0_ffn_b2': (0.0, 0.1)}
    factors = {'L0_attn_Wq': 8.0,
     'L0_attn_bq': 8.0,
     'L0_attn_Wk': 8.0,
     'L0_attn_bk': 8.0,
     'L0_attn_Wv': 8.0,
     'L0_attn_bv': 8.0,
     'L0_attn_Wo': 7.612,
     'L0_attn_bo': 3.072}
    for name, (base, spread) in spreads.items():
        noise = np.random.default_rng([zlib.crc32(name.encode()), seed]).standard_normal(out[name].shape)
        drawn = base * np.exp(spread * noise) if base else spread * noise
        out[name] = jnp.asarray(drawn.astype(out[name].dtype))
    for name, factor in factors.items():
        out[name] = (out[name] * factor).astype(out[name].dtype)
    return out
```

```python
from contextlib import ExitStack

import concourse.bass as bass
from concourse import mybir

F32 = mybir.dt.float32
BF16 = mybir.dt.bfloat16
I32 = mybir.dt.int32
U32 = mybir.dt.uint32
ALU = mybir.AluOpType
ACT = mybir.ActivationFunctionType
AX_X = mybir.AxisListType.X
RADD = bass.bass_isa.ReduceOp.add

P = 128
B, S, D = 4, 1024, 256
H, DH = 16, 16
E, DI = 8, 1024
TOK = B * S
TILES = TOK // P
CAP = 2 * TOK // E
KC = D // P
BLK = 512
NBLK = TOK // BLK
BT = BLK // P
HG = 4
GROUPS = B * H // HG
QT = S // P
HALF = S // 2
VW = 32
TERMS = ((0, 0), (0, 1), (1, 0), (0, 2), (2, 0), (1, 1))
SROWS = DH * len(TERMS)
MROWS = 3
ROW = D + E + 1
BITS = 30
FC = DI // P
ST = CAP // P
EPS = 1e-5
SCALE = float(D) ** -0.5
NOWHERE = 100000.0


def build(nc, a, out):
    with ExitStack() as top:
        xrow = nc.dram_tensor("xrow", (TOK, ROW), F32, kind="Internal").ap()
        slots_dram = nc.dram_tensor("slot_rows", (E * CAP, ROW), F32, kind="Internal").ap()
        qs_dram = nc.dram_tensor("q_parts", (3, GROUPS, 2 * HG, DH, HALF), BF16, kind="Internal").ap()
        ks_dram = nc.dram_tensor("k_parts", (3, GROUPS, 2 * HG, DH, HALF), BF16, kind="Internal").ap()
        v_dram = nc.dram_tensor("v_groups", (GROUPS, P, QT, HG * VW), F32, kind="Internal").ap()
        keep = Keep(nc, top)
        with ExitStack() as ctx:
            norm_stage(nc, ctx, a, keep, xrow, qs_dram, ks_dram, v_dram)
        with ExitStack() as ctx:
            attention_stage(nc, ctx, keep, xrow, slots_dram, qs_dram, ks_dram, v_dram)
        with ExitStack() as ctx:
            project_stage(nc, ctx, a, keep, out)
        with ExitStack() as ctx:
            expert_stage(nc, ctx, a, keep, slots_dram, out)


class Keep:

    def __init__(self, nc, ctx):
        def sb(name, shape, dt):
            return ctx.enter_context(nc.sbuf_tensor(name, shape, dt))

        self.ident = sb("ident", [P, P], F32)
        self.identb = sb("identb", [P, P], BF16)
        self.slot = sb("slot", [P, TILES, E], U32)
        self.heads = sb("heads", [P, GROUPS // 2, QT, 2 * HG * DH], F32)
        self.upper = sb("upper", [P, P], BF16)
        self.ones = sb("ones", [P, P], BF16)
        self.prob = sb("prob", [P, TILES, E], F32)
        self.thr = sb("thr", [P, E], I32)
        self.tot = sb("tot", [P, E], F32)
        self.wo = sb("wo", [P, KC, D], F32)
        self.bo = sb("bo", [P, D], F32)
        self.psum = ctx.enter_context(nc.psum_tensor("psum", [P, 8, 512], F32))


def norm_stage(nc, ctx, a, keep, xrow, qs_dram, ks_dram, v_dram):
    def sb(name, shape, dt=F32):
        return ctx.enter_context(nc.sbuf_tensor(name, shape, dt))

    def sem(name):
        return ctx.enter_context(nc.semaphore(name))

    ps = keep.psum
    xin = sb("xin", [P, 2, BT, D])
    row = sb("row", [P, 2, BT, ROW])
    stats = sb("stats", [P, 2, BT, 6])
    mean_var = sb("mean_var", [P, 2, BT, 2])
    var_eps = sb("var_eps", [P, 2, BT])
    std = sb("std", [P, 2, BT])
    rstd = sb("rstd", [P, 2, BT])
    xt = sb("xt", [P, 2, KC, BLK])
    xnt = sb("xnt", [P, KC, TOK])
    wvr = sb("wvr", [P, KC, D + E])
    wqk = sb("wqk", [P, 2, KC, D])
    bqk = sb("bqk", [P, 2, KC])
    bv = sb("bv", [P, D])
    vst = sb("vst", [P, 2, BT, H, VW])
    lg = sb("lg", [P, 2, BT, E])
    lmax = sb("lmax", [P, 2, BT])
    lsh = sb("lsh", [P, 2, BT, E])
    lexp = sb("lexp", [P, 2, BT, E])
    lsum = sb("lsum", [P, 2, BT])
    lrec = sb("lrec", [P, 2, BT])
    tid_i = sb("tid_i", [P, TILES], I32)
    tid = sb("tid", [P, TILES])
    cos = sb("cos", [P, S])
    sin = sb("sin", [P, S])
    qb = sb("qb", [P, 2, BLK])
    qsw = sb("qsw", [P, 2, BLK])
    qc = sb("qc", [P, 2, BLK])
    qsn = sb("qsn", [P, 2, BLK])
    qr = sb("qr", [P, 2, BLK])
    rest = sb("rest", [P, 2, BLK])
    q1 = sb("q1", [P, 2, BLK], BF16)
    q2 = sb("q2", [P, 2, BLK], BF16)
    q3 = sb("q3", [P, 2, BLK], BF16)
    upper, ones, thr, tot, prob = keep.upper, keep.ones, keep.thr, keep.tot, keep.prob
    bits_i = sb("bits_i", [P, BITS, E], I32)
    bits_f = sb("bits_f", [P, BITS, E])
    cand = sb("cand", [P, E], I32)
    gain = sb("gain", [P, E], I32)
    diff = sb("diff", [P, TILES, E])
    tree = sb("tree", [P, TILES, E])
    took = sb("took", [P, E])

    s_w = sem("s_w")
    s_bits = sem("s_bits")
    s_x = [sem("s_x0"), sem("s_x1")]
    s_stat = sem("s_stat")
    s_var = sem("s_var")
    s_std = sem("s_std")
    s_xn = sem("s_xn")
    s_tr = sem("s_tr")
    s_xt = sem("s_xt")
    s_xnt = sem("s_xnt")
    s_vr = sem("s_vr")
    s_v = sem("s_v")
    s_sh = sem("s_sh")
    s_ex = sem("s_ex")
    s_prob = sem("s_prob")
    s_row = sem("s_row")
    s_store = [sem("s_store0"), sem("s_store1")]
    s_pool = sem("s_pool")
    s_step = sem("s_step")
    s_const = sem("s_const")
    s_one = sem("s_one")
    s_pq = sem("s_pq")
    s_qb = sem("s_qb")
    s_rope = sem("s_rope")
    s_q1 = sem("s_q1")
    s_r1 = sem("s_r1")
    s_q2 = sem("s_q2")
    s_q3 = sem("s_q3")
    s_dve = sem("s_dve")
    s_qst = [sem("s_qst0"), sem("s_qst1")]
    NW = 8

    x_blocks = a["x"].rearrange("b (n t p) d -> (b n) p t d", p=P, t=BT)
    row_blocks = xrow.rearrange("(n t p) c -> n p t c", p=P, t=BT)
    v_blocks = v_dram.rearrange("(b g) p (n t) c -> b n p t g c", g=H // HG, t=BT)
    q_blocks = [t.rearrange("a (b m g) (n j) r s -> a b m n g (j r) s", b=B, m=KC, n=S // BLK) for t in (qs_dram, ks_dram)]

    with nc.Block() as block:
        @block.sync
        def _(sp):
            sp.dma_start(keep.ident[:, :], a["c_ident"]).then_inc(s_w, 16)
            for kc in range(KC):
                rows = slice(kc * P, (kc + 1) * P)
                sp.dma_start(wvr[:, kc, 0:D], a["Wv"][rows, :]).then_inc(s_w, 16)
                sp.dma_start(wvr[:, kc, D:D + E], a["Wr"][rows, :]).then_inc(s_w, 16)
            sp.dma_start(bv[:, :], a["bv"].partition_broadcast(P)).then_inc(s_w, 16)

            def load_x(i, k):
                sp.dma_start(xin[:, k, :, :], x_blocks[i * 2 + k]).then_inc(s_x[k], 16)

            for k in range(2):
                load_x(0, k)
            for q, (w, b) in enumerate((("Wq", "bq"), ("Wk", "bk"))):
                sp.dma_start(wqk[:, q, :, :], a[w].rearrange("(c p) n -> p c n", p=P)).then_inc(s_w, 16)
                sp.dma_start(bqk[:, q, :], a[b]).then_inc(s_qst[q], 16)
            sp.dma_start(cos[:, :], a["c_cos"]).then_inc(s_store[0], 16)
            sp.dma_start(sin[:, :], a["c_sin"]).then_inc(s_store[1], 16)

            def store_block(b, k):
                sp.wait_ge(s_row, 1)
                sp.sem_inc(s_row, -1)
                sp.dma_start(row_blocks[b * 2 + k], row[:, k, :, :]).then_inc(s_store[k], 16)
                for g in range(H // HG):
                    sp.dma_start(v_blocks[b, k, :, :, g, :],
                                 vst[:, k, :, g * HG:(g + 1) * HG, :].rearrange("p t h w -> p t (h w)")).then_inc(s_store[k], 16)

            with sp.Fori(0, NBLK // 2 - 1) as i:
                for k in range(2):
                    store_block(i, k)
                    load_x(i + 1, k)
            for k in range(2):
                store_block(NBLK // 2 - 1, k)

            with sp.Fori(0, B) as b:
                for n in range(S // BLK):
                    for q in range(2):
                        for m in range(KC):
                            r = (n * 2 + q) * KC + m
                            k = r % 2
                            sp.wait_ge(s_q3, b * 8 + (r + 1))
                            for part, tile in enumerate((q1, q2, q3)):
                                for g in range(2):
                                    sp.dma_start(q_blocks[q][part, b, m, n, g],
                                                 tile[g * HG * DH:(g + 1) * HG * DH, k, :]).then_inc(s_qst[k], 16)
            for k in range(2):
                sp.wait_ge(s_store[k], NBLK // 2 * 5 * 16 + 16)
                sp.wait_ge(s_qst[k], B * 4 * 6 * 16 + 16)

        @block.gpsimd
        def _(pool):
            pool.dma_start(bits_i[:, :, :], a["c_bits"].partition_broadcast(P)).then_inc(s_bits, 16)
            pool.memset(ones[:, :], 1.0).then_inc(s_pool, 1)
            pool.iota(tid_i[:, :], [[P, TILES]], 0, channel_multiplier=1).then_inc(s_pool, 1)
            pool.wait_ge(s_pool, 2)
            pool.affine_select(out=upper[:, :], in_=ones[:, :], compare_op=ALU.is_gt, fill=0.0, base=0,
                               pattern=[[1, P]], channel_multiplier=-1).then_inc(s_const, 1)
            pool.tensor_copy(tid[:, :], tid_i[:, :]).then_inc(s_const, 1)
            pool.wait_ge(s_w, 16 * NW)
            pool.wait_ge(s_bits, 16)
            pool.tensor_copy(keep.identb[:, :], keep.ident[:, :]).then_inc(s_const, 1)
            pool.tensor_copy(bits_f[:, :, :], bits_i[:, :, :]).then_inc(s_const, 1)
            pool.memset(thr[:, :], 0).then_inc(s_const, 1)
            pool.wait_ge(s_const, 5)
            pool.wait_ge(s_prob, 2 * NBLK)
            STEPS = 13
            with pool.Fori(0, BITS) as i:
                def chained(instruction, step):
                    instruction.then_inc(s_step, 1)
                    pool.wait_ge(s_step, step)

                chained(pool.tensor_tensor(cand[:, :], thr[:, :], bits_i[:, bass.ds(i, 1), :].rearrange("p o e -> p (o e)"), ALU.add), 1)
                chained(pool.tensor_tensor(diff[:, :, :], prob[:, :, :],
                                           cand[:, :].bitcast(F32).unsqueeze(1).to_broadcast([P, TILES, E]),
                                           ALU.subtract), 2)
                chained(pool.tensor_scalar(tree[:, :, :], diff[:, :, :], 0.0, None, ALU.is_ge), 3)
                chained(pool.tensor_tensor(tree[:, 0:16, :], tree[:, 0:16, :], tree[:, 16:32, :], ALU.add), 4)
                chained(pool.tensor_tensor(tree[:, 0:8, :], tree[:, 0:8, :], tree[:, 8:16, :], ALU.add), 5)
                chained(pool.tensor_tensor(tree[:, 0:4, :], tree[:, 0:4, :], tree[:, 4:8, :], ALU.add), 6)
                chained(pool.tensor_tensor(tree[:, 0:2, :], tree[:, 0:2, :], tree[:, 2:4, :], ALU.add), 7)
                chained(pool.tensor_tensor(tree[:, 0, :], tree[:, 0, :], tree[:, 1, :], ALU.add), 8)
                chained(pool.partition_all_reduce(tot[:, :], tree[:, 0, :], P, RADD), 9)
                chained(pool.tensor_scalar(took[:, :], tot[:, :], float(CAP), None, ALU.is_ge), 10)
                chained(pool.tensor_tensor(took[:, :], took[:, :], bits_f[:, bass.ds(i, 1), :].rearrange("p o e -> p (o e)"), ALU.mult), 11)
                chained(pool.tensor_copy(gain[:, :], took[:, :]), 12)
                chained(pool.tensor_tensor(thr[:, :], thr[:, :], gain[:, :], ALU.add), 13)
                pool.sem_inc(s_step, -STEPS)
        @block.vector
        def _(dve):
            dve.memset(vst[:, :, :, :, :], 1.0).then_inc(s_one, 1)
            dve.sem_inc(s_v, 2)
            dve.wait_ge(s_one, 1)
            dve.wait_ge(s_const, 5)
            dve.wait_ge(s_w, 16 * NW)
            with dve.Fori(0, NBLK // 2) as i:
                for k in range(2):
                    n = i * 2 + k
                    dve.wait_ge(s_x[k], i * 16 + 16)
                    for t in range(BT):
                        dve.bn_stats(stats[:, k, t, :], xin[:, k, t, :]).then_inc(s_stat, 1)
                    dve.wait_ge(s_stat, BT)
                    for t in range(BT):
                        dve.bn_aggr(mean_var[:, k, t, :], stats[:, k, t, :]).then_inc(s_stat, 1)
                    dve.wait_ge(s_stat, 2 * BT)
                    dve.tensor_scalar(var_eps[:, k, :], mean_var[:, k, :, 1], EPS, None, ALU.add).then_inc(s_var, 1)
                    dve.wait_ge(s_std, n + 1)
                    dve.reciprocal(rstd[:, k, :], std[:, k, :]).then_inc(s_stat, 1)
                    dve.wait_ge(s_stat, 2 * BT + 1)
                    dve.wait_ge(s_store[k], i * 80 + 16)
                    for t in range(BT):
                        last = dve.tensor_scalar(row[:, k, t, 0:D], xin[:, k, t, :], mean_var[:, k, t, 0:1],
                                                 rstd[:, k, t:t + 1], ALU.subtract, ALU.mult)
                    last.then_inc(s_xn, 1)
                    for t in range(BT):
                        dve.wait_ge(s_vr, n * BT + (t + 1))
                        dve.tensor_tensor(vst[:, k, t, :, 0:DH], ps[:, 4 + t % 2, 0:D].rearrange("p (h d) -> p h d", h=H),
                                          bv[:, :].rearrange("p (h d) -> p h d", h=H), ALU.add)
                        dve.tensor_copy(lg[:, k, t, :], ps[:, 4 + t % 2, D:D + E]).then_inc(s_v, 1)
                    dve.wait_ge(s_v, n * BT + (BT + 2))
                    dve.tensor_reduce(lmax[:, k, :], lg[:, k, :, :], AX_X, ALU.max).then_inc(s_stat, 1)
                    dve.wait_ge(s_stat, 2 * BT + 2)
                    dve.tensor_tensor(lsh[:, k, :, :], lg[:, k, :, :],
                                      lmax[:, k, :].unsqueeze(2).to_broadcast([P, BT, E]), ALU.subtract).then_inc(s_sh, 1)
                    dve.wait_ge(s_ex, n + 1)
                    dve.tensor_reduce(lsum[:, k, :], lexp[:, k, :, :], AX_X, ALU.add).then_inc(s_stat, 1)
                    dve.wait_ge(s_stat, 2 * BT + 3)
                    dve.reciprocal(lrec[:, k, :], lsum[:, k, :]).then_inc(s_stat, 1)
                    dve.wait_ge(s_stat, 2 * BT + 4)
                    dve.sem_inc(s_stat, -(2 * BT + 4))
                    dve.tensor_tensor(row[:, k, :, D:D + E], lexp[:, k, :, :],
                                      lrec[:, k, :].unsqueeze(2).to_broadcast([P, BT, E]), ALU.mult).then_inc(s_prob, 1)
                    dve.tensor_tensor(prob[:, bass.ds(n * BT, BT), :], lexp[:, k, :, :],
                                      lrec[:, k, :].unsqueeze(2).to_broadcast([P, BT, E]), ALU.mult).then_inc(s_prob, 1)
                    dve.tensor_copy(row[:, k, :, ROW - 1], tid[:, bass.ds(n * BT, BT)]).then_inc(s_row, 1)
            swap = [j ^ 1 for j in range(32)]
            for k in range(2):
                dve.wait_ge(s_store[k], 16)
            with dve.Fori(0, B) as b:
                for r in range(8):
                    k = r % 2
                    n = b * 8 + r
                    pos = slice(BLK * (r // 4), BLK * (r // 4) + BLK)
                    dve.wait_ge(s_qb, n + 3)
                    dve.tensor_tensor(qc[:, k, :], qb[:, k, :], cos[:, pos], ALU.mult).then_inc(s_dve, 1)
                    dve.stream_shuffle(qsw[:, k, :], qb[:, k, :], swap).then_inc(s_dve, 1)
                    dve.wait_ge(s_dve, n * 3 + 2)
                    dve.tensor_tensor(qsn[:, k, :], qsw[:, k, :], sin[:, pos], ALU.mult).then_inc(s_dve, 1)
                    dve.wait_ge(s_dve, n * 3 + 3)
                    dve.tensor_tensor(qr[:, k, :], qc[:, k, :], qsn[:, k, :], ALU.add).then_inc(s_rope, 1)
                    dve.wait_ge(s_q1, n + 1)
                    dve.tensor_tensor(rest[:, k, :], qr[:, k, :], q1[:, k, :], ALU.subtract).then_inc(s_r1, 1)
                    dve.wait_ge(s_q2, n + 1)
                    dve.tensor_tensor(q3[:, k, :], rest[:, k, :], q2[:, k, :], ALU.subtract).then_inc(s_q3, 1)

        @block.scalar
        def _(act):
            act.sem_inc(s_xnt, 1)
            act.sem_inc(s_qb, 2)
            with act.Fori(0, NBLK // 2) as i:
                for k in range(2):
                    n = i * 2 + k
                    act.wait_ge(s_var, n + 1)
                    act.activation(std[:, k, :], var_eps[:, k, :], ACT.Sqrt).then_inc(s_std, 1)
                    act.wait_ge(s_tr, n * 2 + 1)
                    act.copy(xt[:, k, 0, :], ps[:, k * 2, :]).then_inc(s_xt, 1)
                    act.wait_ge(s_tr, n * 2 + 2)
                    act.copy(xt[:, k, 1, :], ps[:, k * 2 + 1, :]).then_inc(s_xt, 1)
                    for kc in range(KC):
                        act.copy(xnt[:, kc, bass.ds(n * BLK, BLK)], ps[:, k * 2 + kc, :]).then_inc(s_xnt, 1)
                    act.wait_ge(s_sh, n + 1)
                    act.activation(lexp[:, k, :, :], lsh[:, k, :, :], ACT.Exp).then_inc(s_ex, 1)
            for q in range(2):
                act.wait_ge(s_qst[q], 16)
            with act.Fori(0, B) as b:
                for r in range(8):
                    k, q, m = r % 2, r // 2 % 2, r % 2
                    n = b * 8 + r
                    act.wait_ge(s_pq, n + 1)
                    act.activation(qb[:, k, :], ps[:, k, :], ACT.Identity, bias=bqk[:, q, m:m + 1]).then_inc(s_qb, 1)
                    act.wait_ge(s_rope, n + 1)
                    act.wait_ge(s_qst[k], b * 384 + (96 * (r // 2) + 16))
                    act.copy(q1[:, k, :], qr[:, k, :]).then_inc(s_q1, 1)
                    act.wait_ge(s_r1, n + 1)
                    act.copy(q2[:, k, :], rest[:, k, :]).then_inc(s_q2, 1)

        @block.tensor
        def _(pe):
            pe.wait_ge(s_w, 16 * NW)
            with pe.Fori(0, NBLK // 2) as i:
                for k in range(2):
                    n = i * 2 + k
                    pe.wait_ge(s_xn, n + 1)
                    pe.wait_ge(s_xnt, i * (2 * KC) + 1)
                    for kc in range(KC):
                        for t in range(BT):
                            last = pe.transpose(ps[:, k * 2 + kc, t * P:(t + 1) * P],
                                                row[:, k, t, kc * P:(kc + 1) * P], keep.ident[:, :])
                        last.then_inc(s_tr, 1)
                    pe.wait_ge(s_xt, n * 2 + 2)
                    for t in range(BT):
                        pe.wait_ge(s_v, n * BT + (t + 1))
                        for kc in range(KC):
                            last = pe.matmul(ps[:, 4 + t % 2, 0:D + E], xt[:, k, kc, t * P:(t + 1) * P],
                                             wvr[:, kc, :], start=(kc == 0), stop=(kc == KC - 1))
                        last.then_inc(s_vr, 1)
            with pe.Fori(0, B) as b:
                pe.wait_ge(s_xnt, KC * NBLK + 1)
                for r in range(8):
                    k, blk, q, m = r % 2, r // 4, r // 2 % 2, r % 2
                    pe.wait_ge(s_qb, b * 8 + (r + 1))
                    for kc in range(KC):
                        last = pe.matmul(ps[:, k, :], wqk[:, q, kc, m * P:(m + 1) * P],
                                         xnt[:, kc, bass.ds(b * S + blk * BLK, BLK)],
                                         start=(kc == 0), stop=(kc == KC - 1))
                    last.then_inc(s_pq, 1)


def attention_stage(nc, ctx, keep, xrow, slots_dram, qs_dram, ks_dram, v_dram):
    def sb(name, shape, dt=F32):
        return ctx.enter_context(nc.sbuf_tensor(name, shape, dt))

    def sem(name):
        return ctx.enter_context(nc.semaphore(name))

    ps = keep.psum
    SB, TB, OB = 0, 4, 6
    qst = sb("qst", [P, 2, 2, HG, HALF], BF16)
    kst = sb("kst", [P, 2, 2, HG, HALF], BF16)
    vgr = sb("vgr", [P, 2, QT, HG * VW])
    pt = sb("pt", [P, 2, HG, HALF])
    mx = sb("mx", [P, 2, HG, QT // 2])
    negm = sb("negm", [P, 2, 2 * MROWS, HG, QT // 2], BF16)
    mrest = sb("mrest", [P, 2, HG, QT // 2])
    mrow = sb("mrow", [MROWS * HG * QT // 2, 2, P], BF16)
    osb = sb("osb", [P, 2, HALF])
    den = sb("den", [P, 2, QT // 2, HG])
    stage = sb("stage", [P, 2, ROW])
    where = sb("where", [P, 2, E], U32)

    prob, thr, tot = keep.prob, keep.thr, keep.tot
    diff = sb("a_diff", [P, TILES, E])
    mask = sb("mask", [P, 2, TILES, E], BF16)
    inside = sb("inside", [P, 2, TILES, E])
    off0 = sb("off0", [P, 2, TILES, E])
    off1 = sb("off1", [P, 2, TILES, E])
    rank = sb("rank", [P, 2, TILES, E])
    fits = sb("fits", [P, TILES, E])
    slot_f = sb("slot_f", [P, TILES, E])
    slot_t = sb("slot_t", [P, TILES, E])

    s_slot = sem("s_slot")
    s_mask = sem("s_mask")
    s_pre = sem("s_pre")
    s_ins = sem("s_ins")
    in_stack = [sem("in_stack0"), sem("in_stack1")]
    s_const = sem("a_const")
    st_ready = sem("st_ready")
    exp_done = sem("exp_done")
    pv_done = sem("pv_done")
    s_ready = sem("s_ready")
    max_done = sem("max_done")
    split = sem("split")
    neg_ready = sem("neg_ready")
    neg_t = sem("neg_t")
    mrow_ready = sem("mrow_ready")
    mrow_in = [sem("mrow_in0"), sem("mrow_in1")]
    o_copied = sem("o_copied")
    o_t = sem("o_t")
    o_rec = sem("o_rec")
    o_norm = sem("o_norm")
    in_row = [sem("in_row0"), sem("in_row1")]
    s_freed = sem("s_freed")
    s_where = sem("s_where")
    sent = [sem("sent0"), sem("sent1")]
    UNITS = 2 * QT
    LAG = 4
    NLOAD = 2 * len(TERMS) + 1
    TURN_A, TURN_B = 13, 5

    with nc.Block() as block:
        @block.sync
        def _(sp):
            def load_stack(g, par):
                for r, (pq, pk) in enumerate(TERMS):
                    rows = slice(r * DH, (r + 1) * DH)
                    sp.dma_start(qst[rows, par, :, :, :].rearrange("r h j s -> r (h j) s"),
                                 qs_dram[pq, g].rearrange("q r s -> r q s")).then_inc(in_stack[par], 16)
                    sp.dma_start(kst[rows, par, :, :, :].rearrange("r h j s -> r (h j) s"),
                                 ks_dram[pk, g].rearrange("q r s -> r q s")).then_inc(in_stack[par], 16)
                sp.dma_start(vgr[:, par, :, :], v_dram[g]).then_inc(in_stack[par], 16)

            def put_max(g, par, half):
                sp.wait_ge(mrow_ready, g * 2 + (half + 1))
                n = HG * QT // 2
                for part in range(MROWS):
                    sp.dma_start(qst[SROWS + part:SROWS + part + 1, par, half, :, :].rearrange("o j (q t) -> o (j q) t", t=P),
                                 mrow[part * n:(part + 1) * n, half, :]).then_inc(mrow_in[half], 16)

            load_stack(0, 0)
            load_stack(1, 1)
            put_max(0, 0, 0)
            put_max(0, 0, 1)

            def group(g, par):
                put_max(g + 1, 1 - par, 0)
                sp.wait_ge(pv_done, g * UNITS + UNITS)
                load_stack(g + 2, par)
                put_max(g + 1, 1 - par, 1)

            with sp.Fori(0, (GROUPS - 2) // 2) as i:
                for par in range(2):
                    group(i * 2 + par, par)
            put_max(GROUPS - 1, 1, 0)
            put_max(GROUPS - 1, 1, 1)

        @block.gpsimd
        def _(pool):
            rows = xrow.rearrange("(t p) c -> t p c", p=P)

            def load(t, par):
                pool.dma_start(stage[:, par, :], rows[t]).then_inc(in_row[par], 16)

            load(0, 0)
            load(1, 1)
            done = [0]

            def chain(instruction):
                done[0] += 1
                instruction.then_inc(s_slot, 1)
                pool.wait_ge(s_slot, done[0])

            chain(pool.tensor_tensor(diff[:, :, :], prob[:, :, :],
                                     thr[:, :].bitcast(F32).unsqueeze(1).to_broadcast([P, TILES, E]), ALU.subtract))
            pool.tensor_scalar(mask[:, 0, :, :], diff[:, :, :], 0.0, None, ALU.is_gt).then_inc(s_mask, 1)
            pool.tensor_scalar(mask[:, 1, :, :], diff[:, :, :], 0.0, None, ALU.is_equal).then_inc(s_mask, 1)
            pool.wait_ge(s_ins, 4)
            src, dst = off0, off1
            for shift in (1, 2, 4, 8, 16):
                chain(pool.tensor_copy(dst[:, :, 0:shift, :], src[:, :, 0:shift, :]))
                chain(pool.tensor_tensor(dst[:, :, shift:TILES, :], src[:, :, shift:TILES, :],
                                         src[:, :, 0:TILES - shift, :], ALU.add))
                src, dst = dst, src
            chain(pool.tensor_tensor(rank[:, :, :, :], src[:, :, :, :], inside[:, :, :, :], ALU.add))
            above = dst
            chain(pool.tensor_tensor(above[:, 0, 0, :], rank[:, 0, TILES - 1, :], mask[:, 0, TILES - 1, :], ALU.add))
            chain(pool.affine_select(out=above[:, 0, 1, :], in_=above[:, 0, 0, :], compare_op=ALU.is_ge, fill=0.0,
                                     base=-(P - 1), pattern=[[0, E]], channel_multiplier=1))
            chain(pool.partition_all_reduce(tot[:, :], above[:, 0, 1, :], P, RADD))
            chain(pool.tensor_tensor(rank[:, 1, :, :], rank[:, 1, :, :],
                                     tot[:, :].unsqueeze(1).to_broadcast([P, TILES, E]), ALU.add))
            chain(pool.tensor_scalar(fits[:, :, :], rank[:, 1, :, :], float(CAP), None, ALU.is_lt))
            chain(pool.tensor_tensor(fits[:, :, :], fits[:, :, :], mask[:, 1, :, :], ALU.mult))
            for e in range(E):
                chain(pool.tensor_scalar(rank[:, :, :, e], rank[:, :, :, e], float(CAP * e) - NOWHERE, None, ALU.add))
            chain(pool.tensor_tensor(slot_f[:, :, :], rank[:, 0, :, :], mask[:, 0, :, :], ALU.mult))
            chain(pool.tensor_tensor(slot_t[:, :, :], rank[:, 1, :, :], fits[:, :, :], ALU.mult))
            chain(pool.tensor_tensor(slot_f[:, :, :], slot_f[:, :, :], slot_t[:, :, :], ALU.add))
            chain(pool.tensor_scalar(keep.slot[:, :, :], slot_f[:, :, :], NOWHERE, None, ALU.add))

            def scatter(i, par):
                pool.tensor_copy(where[:, par, :], keep.slot[:, bass.ds(i * 2 + par, 1), :].rearrange("p o e -> p (o e)"))\
                    .then_inc(s_where, 1)
                pool.wait_ge(s_where, 1)
                pool.wait_ge(in_row[par], i * 16 + 16)
                pool.sem_inc(s_where, -1)
                for e in range(E):
                    pool.indirect_dma_start(
                        out=slots_dram[:, :], out_offset=bass.IndirectOffsetOnAxis(ap=where[:, par, e:e + 1], axis=0),
                        in_=stage[:, par, :], in_offset=None, bounds_check=E * CAP - 1, oob_is_err=False,
                    ).then_inc(sent[par], 16)

            with pool.Fori(0, TILES // 2 - 1) as i:
                for par in range(2):
                    scatter(i, par)
                for par in range(2):
                    pool.wait_ge(sent[par], i * (16 * E) + 16 * E)
                    pool.sem_inc(s_freed, 1)
                    load(i * 2 + (par + 2), par)
            for par in range(2):
                scatter(TILES // 2 - 1, par)
            for par in range(2):
                pool.wait_ge(sent[par], TILES // 2 * E * 16)

        @block.tensor
        def _(pe):
            def scores_t(g, par, u, half_turn):
                half, kt = u // QT, u % QT
                for j in range(HG):
                    n = g * (UNITS * HG) + (u * HG + j)
                    if j == 0 and u % QT == 0:
                        pe.wait_ge(mrow_in[half], g * (16 * MROWS) + 16 * MROWS)
                    if not (isinstance(g, int) and n < 2):
                        pe.wait_ge(exp_done, n - 1)
                    pe.matmul(ps[:, TB + j % 2, :], kst[0:SROWS + MROWS, par, kt // 4, j, kt % 4 * P:(kt % 4 + 1) * P],
                              qst[0:SROWS + MROWS, par, half, j, :],
                              start=True, stop=True).then_inc(st_ready, 1)
                    yield

            def scores(g, par, s):
                qt, j = s // HG, s % HG
                n = g * (QT * HG) + s
                if not (isinstance(g, int) and n < 2):
                    pe.wait_ge(max_done, n - 1)
                for half in range(2):
                    last = pe.matmul(ps[:, SB + 2 * (s % 2) + half, :], qst[0:SROWS, par, qt // 4, j, qt % 4 * P:(qt % 4 + 1) * P],
                                     kst[0:SROWS, par, half, j, :], start=True, stop=True)
                last.then_inc(s_ready, 1)

            def outputs(g, par, u):
                half, kt = u // QT, u % QT
                if kt == 0:
                    pe.wait_ge(mrow_ready, g * 2 + (half + 1))
                pe.wait_ge(exp_done, g * (UNITS * HG) + (u + 1) * HG)
                for j in range(HG):
                    last = pe.matmul(ps[VW * j:VW * (j + 1), OB + half, :], vgr[:, par, kt, VW * j:VW * (j + 1)],
                                     pt[:, u % 2, j, :], start=(kt == 0), stop=(kt == QT - 1))
                last.then_inc(pv_done, 1)

            def turn_max(g, half):
                n = MROWS * HG * QT // 2
                pe.wait_ge(neg_ready, g * 2 + (half + 1))
                pe.transpose(ps[0:2 * n, OB + half, 0:P // 2].bitcast(BF16),
                             negm[:, half, :, :, :].rearrange("p a j q -> p (a j q)"), keep.identb[:, :]).then_inc(neg_t, 1)

            def turn_outputs(g, half):
                pe.wait_ge(o_copied, g * 2 + (half + 1))
                for t in range(QT // 2):
                    last = pe.transpose(ps[:, OB + half, t * P:(t + 1) * P], osb[:, half, t * P:(t + 1) * P],
                                        keep.ident[:, :])
                last.then_inc(o_t, 1)

            pe.wait_ge(s_mask, 2)
            flat_mask = mask[:, :, :, :].rearrange("p m t e -> p (m t e)")
            pe.matmul(ps[:, OB, :], keep.upper[:, :], flat_mask, start=True, stop=True).then_inc(s_pre, 1)
            pe.matmul(ps[:, OB + 1, :], keep.ones[:, :], flat_mask, start=True, stop=True).then_inc(s_pre, 1)
            pe.wait_ge(s_const, 2)
            pe.wait_ge(in_stack[0], 16 * NLOAD)
            for s in range(QT * HG):
                scores(0, 0, s)
            pe.wait_ge(s_ins, 4)
            turn_max(0, 0)
            for _ in scores_t(0, 0, 0, 0):
                pass

            def tiles_of_scores(g, par, u, first, last):
                if u >= LAG and not last:
                    return [(g + 1, 1 - par, 2 * (u - LAG) + n) for n in range(2)]
                if u < LAG and not first:
                    return [(g, par, 2 * (u + UNITS - LAG) + n) for n in range(2)]
                return []

            def group(g, par, turns, first, last):
                for u in range(UNITS):
                    tiles = tiles_of_scores(g, par, u, first, last)
                    if u == LAG and not last:
                        pe.wait_ge(in_stack[1 - par], turns * (16 * NLOAD) + 16 * NLOAD)
                    if u + 1 < UNITS:
                        ahead = scores_t(g, par, u + 1, 0)
                    else:
                        ahead = scores_t(g + 1, 1 - par, 0, 0) if not last else iter(())
                    next(ahead, None)
                    if tiles:
                        scores(*tiles[0])
                    next(ahead, None)
                    outputs(g, par, u)
                    next(ahead, None)
                    if tiles:
                        scores(*tiles[1])
                    for _ in ahead:
                        pass
                    if u == 2 and not first:
                        turn_outputs(g - 1, 1)
                    if u == TURN_B:
                        if not first:
                            pe.wait_ge(o_norm, g * 2)
                        turn_max(g, 1)
                    if u == QT + 2:
                        turn_outputs(g, 0)
                    if u == TURN_A and not last:
                        pe.wait_ge(o_norm, g * 2 + 1)
                        turn_max(g + 1, 0)

            group(0, 0, 0, True, False)
            with pe.Fori(0, (GROUPS - 2) // 2) as i:
                group(i * 2 + 1, 1, i + 1, False, False)
                group(i * 2 + 2, 0, i + 1, False, False)
            group(GROUPS - 1, 1, None, False, True)
            turn_outputs(GROUPS - 1, 1)

        @block.scalar
        def _(act):
            def rows_of_max(g, half):
                n = MROWS * HG * QT // 2
                act.wait_ge(neg_t, g * 2 + (half + 1))
                if not (isinstance(g, int) and g == 0):
                    act.wait_ge(mrow_in[half], g * (16 * MROWS))
                act.copy(mrow[:, half, :], ps[0:n, OB + half, 0:P // 2].bitcast(BF16)).then_inc(mrow_ready, 1)

            def copy_outputs(g, half):
                act.wait_ge(pv_done, g * UNITS + (half + 1) * QT)
                if not (isinstance(g, int) and g == 0):
                    act.wait_ge(o_t, g * 2 + (half - 1))
                act.copy(osb[:, half, :], ps[:, OB + half, :]).then_inc(o_copied, 1)

            def group(g, first, last):
                for u in range(UNITS):
                    if not (first and u < 2):
                        act.wait_ge(pv_done, g * UNITS + (u - 1))
                    for j in range(HG):
                        act.wait_ge(st_ready, g * (UNITS * HG) + (u * HG + j + 1))
                        act.activation(pt[:, u % 2, j, :], ps[:, TB + j % 2, :], ACT.Exp, scale=SCALE).then_inc(exp_done, 1)
                    if u == 1 and not first:
                        copy_outputs(g - 1, 1)
                    if u == TURN_B + 1:
                        rows_of_max(g, 1)
                    if u == QT + 1:
                        copy_outputs(g, 0)
                    if u == TURN_A + 1 and not last:
                        rows_of_max(g + 1, 0)

            rows_of_max(0, 0)
            group(0, True, False)
            with act.Fori(0, GROUPS - 2) as i:
                group(i + 1, False, False)
            group(GROUPS - 1, False, True)
            copy_outputs(GROUPS - 1, 1)

        @block.vector
        def _(dve):
            dve.memset(kst[SROWS:P, :, :, :, :], 1.0).then_inc(s_const, 1)
            dve.memset(negm[:, :, :, :, :], 0.0).then_inc(s_const, 1)
            dve.memset(off0[:, :, 0, :], 0.0).then_inc(s_ins, 1)
            dve.wait_ge(s_const, 2)
            dve.wait_ge(s_pre, 2)
            dve.tensor_copy(inside[:, :, :, :], ps[:, OB, :].rearrange("p (m t e) -> p m t e", m=2, t=TILES)).then_inc(s_ins, 1)
            totals = ps[:, OB + 1, :].rearrange("p (m t e) -> p m t e", m=2, t=TILES)
            for m in range(2):
                dve.tensor_copy(off0[:, m, 1:TILES, :], totals[:, m, 0:TILES - 1, :]).then_inc(s_ins, 1)

            def take_max(g, s):
                qt, j = s // HG, s % HG
                dve.wait_ge(s_ready, g * (QT * HG) + (s + 1))
                dve.tensor_reduce(mx[:, qt // 4, j, qt % 4:qt % 4 + 1], ps[:, SB + 2 * (s % 2):SB + 2 * (s % 2) + 2, :]
                                  .rearrange("p b n -> p (b n)"), AX_X, ALU.max).then_inc(max_done, 1)

            def split_max(g, half):
                m = mx[:, half, :, :]
                dve.wait_ge(max_done, g * (QT * HG) + (half + 1) * (QT * HG // 2))
                if not (isinstance(g, int) and g == 0):
                    dve.wait_ge(neg_t, g * 2 + (half - 1))
                at = g * 6 + 3 * half
                dve.tensor_scalar(negm[:, half, 0, :, :], m, -1.0, None, ALU.mult).then_inc(split, 1)
                dve.wait_ge(split, at + 1)
                dve.scalar_tensor_tensor(out=mrest[:, half, :, :], in0=m, scalar=-1.0, in1=negm[:, half, 0, :, :],
                                         op0=ALU.mult, op1=ALU.subtract).then_inc(split, 1)
                dve.wait_ge(split, at + 2)
                dve.tensor_copy(negm[:, half, 1, :, :], mrest[:, half, :, :]).then_inc(split, 1)
                dve.wait_ge(split, at + 3)
                dve.tensor_tensor(negm[:, half, 2, :, :], mrest[:, half, :, :], negm[:, half, 1, :, :],
                                  ALU.subtract).then_inc(neg_ready, 1)

            def normalise(pair, par, half):
                g = pair * 2 + par
                o = ps[:, OB + half, :].rearrange("p (t j w) -> p t j w", t=QT // 2, j=HG)
                dve.wait_ge(o_t, g * 2 + (half + 1))
                dve.reciprocal(den[:, half, :, :], o[:, :, :, DH]).then_inc(o_rec, 1)
                dve.wait_ge(o_rec, g * 2 + (half + 1))
                where_to = keep.heads[:, bass.ds(pair, 1), half * (QT // 2):(half + 1) * (QT // 2),
                                      par * HG * DH:(par + 1) * HG * DH]
                dve.tensor_tensor(where_to.rearrange("p o t (j d) -> p (o t) j d", j=HG), o[:, :, :, 0:DH],
                                  den[:, half, :, :].unsqueeze(3).to_broadcast([P, QT // 2, HG, DH]),
                                  ALU.mult).then_inc(o_norm, 1)

            for s in range(QT * HG):
                take_max(0, s)
                if s % 16 == 15:
                    split_max(0, s // 16)

            def group(pair, par, first, last):
                g = pair * 2 + par
                for u in range(UNITS):
                    for n in range(2):
                        if u >= LAG and not last:
                            take_max(g + 1, 2 * (u - LAG) + n)
                        if u < LAG and not first:
                            take_max(g, 2 * (u + UNITS - LAG) + n)
                    if u == LAG + QT - 1 and not last:
                        split_max(g + 1, 0)
                    if u == LAG - 1 and not first:
                        split_max(g, 1)
                    if u == 2 and not first:
                        normalise(pair - (1 - par), 1 - par, 1)
                    if u == QT + 2:
                        normalise(pair, par, 0)

            group(0, 0, True, False)
            with dve.Fori(0, (GROUPS - 2) // 2) as i:
                group(i, 1, False, False)
                group(i + 1, 0, False, False)
            group(GROUPS // 2 - 1, 1, False, True)
            normalise(GROUPS // 2 - 1, 1, 1)


def project_stage(nc, ctx, a, keep, out):
    def sb(name, shape, dt=F32):
        return ctx.enter_context(nc.sbuf_tensor(name, shape, dt))

    def sem(name):
        return ctx.enter_context(nc.semaphore(name))

    ps = keep.psum
    xres = sb("xres", [P, 2, D])
    base = sb("base", [P, 2, D])
    fin = sb("fin", [P, 2, D])
    ht = sb("ht", [P, 2, KC, P])
    s_w = sem("p_w")
    in_x = [sem("p_x0"), sem("p_x1")]
    s_ht = sem("p_turned")
    s_hc = sem("p_copied")
    s_y = sem("p_product")
    s_base = sem("p_base")
    s_fin = sem("p_final")
    stored = [sem("p_stored0"), sem("p_stored1")]
    x_tiles = a["x"].rearrange("b (t p) d -> (b t) p d", p=P)
    out_tiles = out.rearrange("b (t p) d -> (b t) p d", p=P)

    with nc.Block() as block:
        @block.sync
        def _(sp):
            sp.dma_start(keep.wo[:, :, :], a["Wo"].rearrange("(c p) n -> p c n", p=P)).then_inc(s_w, 16)
            sp.dma_start(keep.bo[:, :], a["bo"].partition_broadcast(P)).then_inc(s_w, 16)
            for t in range(TILES):
                if t >= 2:
                    sp.wait_ge(s_base, t - 1)
                sp.dma_start(xres[:, t % 2, :], x_tiles[t]).then_inc(in_x[t % 2], 16)
                if t >= 1:
                    sp.wait_ge(s_fin, t)
                    sp.dma_start(out_tiles[t - 1], fin[:, (t - 1) % 2, :]).then_inc(stored[(t - 1) % 2], 16)
            sp.wait_ge(s_fin, TILES)
            sp.dma_start(out_tiles[TILES - 1], fin[:, 1, :]).then_inc(stored[1], 16)
            for k in range(2):
                sp.wait_ge(stored[k], TILES // 2 * 16)

        @block.tensor
        def _(pe):
            pe.wait_ge(s_w, 32)
            for t in range(TILES):
                b, q, k = t // QT, t % QT, t % 2
                if t >= 2:
                    pe.wait_ge(s_hc, t - 1)
                for kc in range(KC):
                    last = pe.transpose(ps[:, k, kc * P:(kc + 1) * P],
                                        keep.heads[:, b * KC + kc, q, :], keep.ident[:, :])
                last.then_inc(s_ht, 1)
                pe.wait_ge(s_hc, t + 1)
                if t >= 2:
                    pe.wait_ge(s_fin, t - 1)
                for kc in range(KC):
                    last = pe.matmul(ps[:, 2 + k, 0:D], ht[:, k, kc, :], keep.wo[:, kc, :],
                                     start=(kc == 0), stop=(kc == KC - 1))
                last.then_inc(s_y, 1)

        @block.scalar
        def _(act):
            for t in range(TILES):
                k = t % 2
                act.wait_ge(s_ht, t + 1)
                if t >= 2:
                    act.wait_ge(s_y, t - 1)
                act.copy(ht[:, k, :, :].rearrange("p c n -> p (c n)"), ps[:, k, 0:KC * P]).then_inc(s_hc, 1)

        @block.vector
        def _(dve):
            dve.wait_ge(s_w, 32)
            for t in range(TILES):
                k = t % 2
                dve.wait_ge(in_x[k], 16 * (t // 2 + 1))
                dve.tensor_tensor(base[:, k, :], xres[:, k, :], keep.bo[:, :], ALU.add).then_inc(s_base, 1)
                dve.wait_ge(s_y, t + 1)
                dve.wait_ge(s_base, t + 1)
                if t >= 2:
                    dve.wait_ge(stored[k], 16 * (t // 2))
                dve.tensor_tensor(fin[:, k, :], ps[:, 2 + k, 0:D], base[:, k, :], ALU.add).then_inc(s_fin, 1)


def expert_stage(nc, ctx, a, keep, slots_dram, out):
    def sb(name, shape, dt=F32):
        return ctx.enter_context(nc.sbuf_tensor(name, shape, dt))

    def sem(name):
        return ctx.enter_context(nc.semaphore(name))

    ps = keep.psum
    w1 = sb("w1", [P, 2, KC, DI])
    w2 = sb("w2", [P, 2, FC, D])
    b1 = sb("b1", [P, 2, FC])
    b2 = sb("b2", [P, 2, D])
    rows = sb("rows", [P, 2, ST, ROW])
    xt = sb("x_t", [P, KC, CAP])
    ht = sb("h_t", [P, FC, CAP])
    ids = sb("ids", [P, 2, ST], U32)
    ysum = sb("ysum", [P, 2, D])
    yout = sb("yout", [P, 2, D])
    loaded = [sem("e_loaded0"), sem("e_loaded1")]
    turned = sem("e_turned")
    x_in = sem("e_x_in")
    h_ready = sem("e_h_ready")
    h_in = sem("e_h_in")
    y_ready = sem("e_y_ready")
    y_sum = sem("e_y_sum")
    y_out = sem("e_y_out")
    s_ids = sem("e_ids")
    added = [sem("e_added0"), sem("e_added1")]
    NL = 5
    out_rows = out.rearrange("b s d -> (b s) d")
    slot_rows = slots_dram.rearrange("(e t p) c -> e p t c", e=E, p=P)

    with nc.Block() as block:
        @block.sync
        def _(sp):
            for e in range(E):
                k = e % 2
                if e >= 2:
                    sp.wait_ge(y_out, (e - 1) * ST)
                sp.dma_start(rows[:, k, :, :], slot_rows[e]).then_inc(loaded[k], 16)
                sp.dma_start(w1[:, k, :, :], a["W1"][e].rearrange("(c p) n -> p c n", p=P)).then_inc(loaded[k], 16)
                sp.dma_start(b1[:, k, :], a["b1"][e]).then_inc(loaded[k], 16)
                sp.dma_start(w2[:, k, :, :], a["W2"][e].rearrange("(c p) n -> p c n", p=P)).then_inc(loaded[k], 16)
                sp.dma_start(b2[:, k, :], a["b2"][e].partition_broadcast(P)).then_inc(loaded[k], 16)

        @block.gpsimd
        def _(pool):
            for e in range(E):
                k = e % 2
                pool.wait_ge(loaded[k], 16 * NL * (e // 2 + 1))
                if e >= 2:
                    pass
                pool.tensor_copy(ids[:, k, :], rows[:, k, :, ROW - 1]).then_inc(s_ids, 1)
                pool.wait_ge(s_ids, e + 1)
                if e >= 1:
                    for p in range(2):
                        pool.wait_ge(added[p], 16 * e * ST // 2)
                for t in range(ST):
                    n = e * ST + t
                    pool.wait_ge(y_out, n + 1)
                    pool.indirect_dma_start(
                        out=out_rows, out_offset=bass.IndirectOffsetOnAxis(ap=ids[:, k, t:t + 1], axis=0),
                        in_=yout[:, t % 2, :], in_offset=None, bounds_check=TOK - 1, compute_op=ALU.add,
                    ).then_inc(added[t % 2], 16)
            for p in range(2):
                pool.wait_ge(added[p], 16 * E * ST // 2)

        @block.tensor
        def _(pe):
            for e in range(E):
                k = e % 2
                pe.wait_ge(loaded[k], 16 * NL * (e // 2 + 1))
                for b in range(4):
                    kc, half = b // 2, b % 2
                    n = e * 4 + b
                    if n >= 2:
                        pe.wait_ge(x_in, n - 1)
                    for t in range(4):
                        last = pe.transpose(ps[:, 6 + b % 2, t * P:(t + 1) * P],
                                            rows[:, k, half * 4 + t, kc * P:(kc + 1) * P], keep.ident[:, :])
                    last.then_inc(turned, 1)
                pe.wait_ge(x_in, e * 4 + 4)
                for f in range(FC):
                    n = e * FC + f
                    if n >= 2:
                        pe.wait_ge(h_in, n - 1)
                    for half in range(2):
                        for kc in range(KC):
                            last = pe.matmul(ps[:, 2 * (f % 2) + half, :], w1[:, k, kc, f * P:(f + 1) * P],
                                             xt[:, kc, half * 512:(half + 1) * 512], start=(kc == 0), stop=(kc == KC - 1))
                    last.then_inc(h_ready, 1)
                pe.wait_ge(h_in, (e + 1) * FC)
                for t in range(ST):
                    n = e * ST + t
                    if n >= 2:
                        pe.wait_ge(y_sum, n - 1)
                    for f in range(FC):
                        last = pe.matmul(ps[:, 4 + t % 2, 0:D], ht[:, f, t * P:(t + 1) * P], w2[:, k, f, :],
                                         start=(f == 0), stop=(f == FC - 1))
                    last.then_inc(y_ready, 1)

        @block.scalar
        def _(act):
            for e in range(E):
                k = e % 2
                if e >= 1:
                    act.wait_ge(y_ready, e * ST)
                for f in range(FC):
                    act.wait_ge(h_ready, e * FC + f + 1)
                    act.activation(ht[:, f, :].rearrange("p (b n) -> p b n", b=2), ps[:, 2 * (f % 2):2 * (f % 2) + 2, :],
                                   ACT.Gelu, bias=b1[:, k, f:f + 1]).then_inc(h_in, 1)

        @block.vector
        def _(dve):
            for e in range(E):
                k = e % 2
                if e >= 1:
                    dve.wait_ge(h_ready, e * FC)
                for b in range(4):
                    kc, half = b // 2, b % 2
                    dve.wait_ge(turned, e * 4 + b + 1)
                    dve.tensor_copy(xt[:, kc, half * 512:(half + 1) * 512], ps[:, 6 + b % 2, :]).then_inc(x_in, 1)
                for t in range(ST):
                    n = e * ST + t
                    dve.wait_ge(y_ready, n + 1)
                    if n >= 2:
                        dve.wait_ge(y_out, n - 1)
                    dve.tensor_tensor(ysum[:, t % 2, :], ps[:, 4 + t % 2, 0:D], b2[:, k, :], ALU.add).then_inc(y_sum, 1)
                    dve.wait_ge(y_sum, n + 1)
                    if n >= 2:
                        dve.wait_ge(added[t % 2], 16 * (n // 2))
                    for e2 in range(1):
                        dve.tensor_scalar(yout[:, t % 2, :], ysum[:, t % 2, :], rows[:, k, t, D + e:D + e + 1], None,
                                          ALU.mult).then_inc(y_out, 1)


_NAMES = {"x": "L0_attn_x", "Wq": "L0_attn_Wq", "bq": "L0_attn_bq", "Wk": "L0_attn_Wk", "bk": "L0_attn_bk",
          "Wv": "L0_attn_Wv", "bv": "L0_attn_bv", "Wo": "L0_attn_Wo", "bo": "L0_attn_bo", "Wr": "L0_ffn_Wr",
          "W1": "L0_ffn_W1", "b1": "L0_ffn_b1", "W2": "L0_ffn_W2", "b2": "L0_ffn_b2"}


def constants(np):
    freq = (np.float32(1.0) / np.float32(10000.0) ** (np.arange(0, DH, 2, dtype=np.float32) / np.float32(DH))).astype(np.float32)
    angle = (np.arange(S, dtype=np.float32)[None, :] * freq[:, None]).astype(np.float32)
    angle = np.tile(np.repeat(angle, 2, axis=0), (P // DH, 1))
    sign = np.where(np.arange(P) % 2 == 0, -1.0, 1.0).astype(np.float32)[:, None]
    bits = np.repeat((1 << np.arange(BITS - 1, -1, -1)).astype(np.int32)[:, None], E, axis=1)
    return {"c_ident": np.eye(P, dtype=np.float32), "c_cos": np.cos(angle).astype(np.float32),
            "c_sin": (np.sin(angle) * sign).astype(np.float32), "c_bits": bits}


def kernel(**inputs):
    import numpy as _np
    import concourse.bacc as _bacc
    from concourse import mybir as _mybir
    from concourse.bass_utils import run_bass_kernel_spmd as _run

    nc = _bacc.Bacc("TRN2", target_bir_lowering=False, num_devices=1)
    arrays, aps = {}, {}
    given = {short: _np.ascontiguousarray(inputs[name]) for short, name in _NAMES.items()}
    for name, chunks in (("bq", KC), ("bk", KC)):
        given[name] = _np.ascontiguousarray(given[name].reshape(chunks, P).T)
    given["b1"] = _np.ascontiguousarray(given["b1"].reshape(E, FC, P).transpose(0, 2, 1))
    for name, a in {**given, **constants(_np)}.items():
        arrays[f"in_{name}"] = a
        aps[name] = nc.dram_tensor(f"in_{name}", a.shape, _mybir.dt.from_np(a.dtype), kind="ExternalInput").ap()
    out = nc.dram_tensor("out_0", (B, S, D), _mybir.dt.float32, kind="ExternalOutput").ap()
    build(nc, aps, out)
    r = _run(nc, [arrays], core_ids=[0])
    return r.results[0]["out_0"]
```

```python
from contextlib import ExitStack

import concourse.bass as bass
from concourse import mybir

F32 = mybir.dt.float32
BF16 = mybir.dt.bfloat16
F32R = mybir.dt.float32r
I32 = mybir.dt.int32
U32 = mybir.dt.uint32
ALU = mybir.AluOpType
ACT = mybir.ActivationFunctionType
AX_X = mybir.AxisListType.X
RADD = bass.bass_isa.ReduceOp.add

P = 128
B, S, D = 4, 1024, 256
H, DH = 16, 16
E, DI = 8, 1024
TOK = B * S
TILES = TOK // P
CAP = 2 * TOK // E
KC = D // P
BLK = 512
NBLK = TOK // BLK
BT = BLK // P
HG = 4
GROUPS = B * H // HG
QT = S // P
HALF = S // 2
VW = 32
TERMS = ((0, 0), (0, 1), (1, 0), (0, 2), (2, 0), (1, 1))
SROWS = DH * len(TERMS)
MROWS = 3
ROW = D + E + 1
FIRST_BITS = 20
BITS = 30
FC = DI // P
ST = CAP // P
EPS = 1e-5
SCALE = float(D) ** -0.5
NOWHERE = 100000.0


def build(nc, a, out):
    with ExitStack() as top:
        xrow = nc.dram_tensor("xrow", (TOK, ROW), F32, kind="Internal").ap()
        slots_dram = nc.dram_tensor("slot_rows", (E * CAP, ROW), F32, kind="Internal").ap()
        qs_dram = nc.dram_tensor("q_parts", (3, GROUPS, 2 * HG, DH, HALF), BF16, kind="Internal").ap()
        ks_dram = nc.dram_tensor("k_parts", (3, GROUPS, 2 * HG, DH, HALF), BF16, kind="Internal").ap()
        v_dram = nc.dram_tensor("v_groups", (GROUPS, P, QT, HG * VW), F32, kind="Internal").ap()
        keep = Keep(nc, top)
        with ExitStack() as ctx:
            norm_stage(nc, ctx, a, keep, xrow, qs_dram, ks_dram, v_dram)
        with ExitStack() as ctx:
            attention_stage(nc, ctx, keep, xrow, slots_dram, qs_dram, ks_dram, v_dram)
        with ExitStack() as ctx:
            project_stage(nc, ctx, a, keep, out)
        with ExitStack() as ctx:
            expert_stage(nc, ctx, a, keep, slots_dram, out)


class Keep:

    def __init__(self, nc, ctx):
        def sb(name, shape, dt):
            return ctx.enter_context(nc.sbuf_tensor(name, shape, dt))

        self.ident = sb("ident", [P, P], F32)
        self.identb = sb("identb", [P, P], BF16)
        self.slot = sb("slot", [P, TILES, E], U32)
        self.heads = sb("heads", [P, GROUPS // 2, QT, 2 * HG * DH], F32)
        self.upper = sb("upper", [P, P], BF16)
        self.ones = sb("ones", [P, P], BF16)
        self.prob = sb("prob", [P, TILES, E], F32)
        self.thr = sb("thr", [P, E], I32)
        self.bits_i = sb("bits_i", [P, BITS, E], I32)
        self.bits_f = sb("bits_f", [P, BITS, E], F32)
        self.tot = sb("tot", [P, E], F32)
        self.wo = sb("wo", [P, KC, D], F32)
        self.bo = sb("bo", [P, D], F32)
        self.psum = ctx.enter_context(nc.psum_tensor("psum", [P, 8, 512], F32))


class Search:

    def __init__(self, ctx, nc, name):
        def sb(what, shape, dt=F32):
            return ctx.enter_context(nc.sbuf_tensor(name + what, shape, dt))

        self.cand = sb("cand", [P, E], I32)
        self.gain = sb("gain", [P, E], I32)
        self.diff = sb("diff", [P, TILES, E])
        self.tree = sb("tree", [P, TILES, E])
        self.took = sb("took", [P, E])
        self.s_step = ctx.enter_context(nc.semaphore(name + "step"))


def find_threshold(pool, keep, search, first_bit, end_bit):
    STEPS = 13
    cand, gain, diff, tree, took, s_step = search.cand, search.gain, search.diff, search.tree, search.took, search.s_step
    thr, tot = keep.thr, keep.tot
    with pool.Fori(first_bit, end_bit) as i:
        def chained(instruction, step):
            instruction.then_inc(s_step, 1)
            pool.wait_ge(s_step, step)

        bit_i = keep.bits_i[:, bass.ds(i, 1), :].rearrange("p o e -> p (o e)")
        bit_f = keep.bits_f[:, bass.ds(i, 1), :].rearrange("p o e -> p (o e)")
        chained(pool.tensor_tensor(cand[:, :], thr[:, :], bit_i, ALU.add), 1)
        chained(pool.tensor_tensor(diff[:, :, :], keep.prob[:, :, :],
                                   cand[:, :].bitcast(F32).unsqueeze(1).to_broadcast([P, TILES, E]),
                                   ALU.subtract), 2)
        chained(pool.tensor_scalar(tree[:, :, :], diff[:, :, :], 0.0, None, ALU.is_ge), 3)
        chained(pool.tensor_tensor(tree[:, 0:16, :], tree[:, 0:16, :], tree[:, 16:32, :], ALU.add), 4)
        chained(pool.tensor_tensor(tree[:, 0:8, :], tree[:, 0:8, :], tree[:, 8:16, :], ALU.add), 5)
        chained(pool.tensor_tensor(tree[:, 0:4, :], tree[:, 0:4, :], tree[:, 4:8, :], ALU.add), 6)
        chained(pool.tensor_tensor(tree[:, 0:2, :], tree[:, 0:2, :], tree[:, 2:4, :], ALU.add), 7)
        chained(pool.tensor_tensor(tree[:, 0, :], tree[:, 0, :], tree[:, 1, :], ALU.add), 8)
        chained(pool.partition_all_reduce(tot[:, :], tree[:, 0, :], P, RADD), 9)
        chained(pool.tensor_scalar(took[:, :], tot[:, :], float(CAP), None, ALU.is_ge), 10)
        chained(pool.tensor_tensor(took[:, :], took[:, :], bit_f, ALU.mult), 11)
        chained(pool.tensor_copy(gain[:, :], took[:, :]), 12)
        chained(pool.tensor_tensor(thr[:, :], thr[:, :], gain[:, :], ALU.add), 13)
        pool.sem_inc(s_step, -STEPS)


def norm_stage(nc, ctx, a, keep, xrow, qs_dram, ks_dram, v_dram):
    def sb(name, shape, dt=F32):
        return ctx.enter_context(nc.sbuf_tensor(name, shape, dt))

    def sem(name):
        return ctx.enter_context(nc.semaphore(name))

    ps = keep.psum
    xin = sb("xin", [P, 2, BT, D])
    row = sb("row", [P, 2, BT, ROW])
    stats = sb("stats", [P, 2, BT, 6])
    mean_var = sb("mean_var", [P, 2, BT, 2])
    var_eps = sb("var_eps", [P, 2, BT])
    std = sb("std", [P, 2, BT])
    rstd = sb("rstd", [P, 2, BT])
    xt = sb("xt", [P, 2, KC, BLK])
    xnt = sb("xnt", [P, KC, TOK])
    wvr = sb("wvr", [P, KC, D + E])
    wqk = sb("wqk", [P, 2, KC, D])
    bqk = sb("bqk", [P, 2, KC])
    bv = sb("bv", [P, D])
    vst = sb("vst", [P, 2, BT, H, VW])
    lg = sb("lg", [P, 2, BT, E])
    lmax = sb("lmax", [P, 2, BT])
    lsh = sb("lsh", [P, 2, BT, E])
    lexp = sb("lexp", [P, 2, BT, E])
    lsum = sb("lsum", [P, 2, BT])
    lrec = sb("lrec", [P, 2, BT])
    tid_i = sb("tid_i", [P, TILES], I32)
    tid = sb("tid", [P, TILES])
    cos = sb("cos", [P, S])
    sin = sb("sin", [P, S])
    qb = sb("qb", [P, 2, BLK])
    qsw = sb("qsw", [P, 2, BLK])
    qc = sb("qc", [P, 2, BLK])
    qsn = sb("qsn", [P, 2, BLK])
    qr = sb("qr", [P, 2, BLK])
    rest = sb("rest", [P, 2, BLK])
    q1 = sb("q1", [P, 2, BLK], BF16)
    q2 = sb("q2", [P, 2, BLK], BF16)
    q3 = sb("q3", [P, 2, BLK], BF16)
    upper, ones, thr, tot, prob = keep.upper, keep.ones, keep.thr, keep.tot, keep.prob
    bits_i, bits_f = keep.bits_i, keep.bits_f
    search = Search(ctx, nc, "early_")

    s_w = sem("s_w")
    s_bits = sem("s_bits")
    s_x = [sem("s_x0"), sem("s_x1")]
    s_stat = sem("s_stat")
    s_soft = sem("s_soft")
    s_var = sem("s_var")
    s_std = sem("s_std")
    s_xn = sem("s_xn")
    s_tr = sem("s_tr")
    s_xt = sem("s_xt")
    s_xnt = sem("s_xnt")
    s_vr = sem("s_vr")
    s_v = sem("s_v")
    s_sh = sem("s_sh")
    s_ex = sem("s_ex")
    s_prob = sem("s_prob")
    s_row = sem("s_row")
    s_store = [sem("s_store0"), sem("s_store1")]
    s_pool = sem("s_pool")
    s_const = sem("s_const")
    s_one = sem("s_one")
    s_pq = sem("s_pq")
    s_qb = sem("s_qb")
    s_rope = sem("s_rope")
    s_q1 = sem("s_q1")
    s_r1 = sem("s_r1")
    s_q2 = sem("s_q2")
    s_q3 = sem("s_q3")
    s_dve = sem("s_dve")
    s_qst = [sem("s_qst0"), sem("s_qst1")]
    NW = 8

    x_blocks = a["x"].rearrange("b (n t p) d -> (b n) p t d", p=P, t=BT)
    row_blocks = xrow.rearrange("(n t p) c -> n p t c", p=P, t=BT)
    v_blocks = v_dram.rearrange("(b g) p (n t) c -> b n p t g c", g=H // HG, t=BT)
    q_blocks = [t.rearrange("a (b m g) (n j) r s -> a b m n g (j r) s", b=B, m=KC, n=S // BLK) for t in (qs_dram, ks_dram)]

    with nc.Block() as block:
        @block.sync
        def _(sp):
            sp.dma_start(keep.ident[:, :], a["c_ident"]).then_inc(s_w, 16)
            for kc in range(KC):
                rows = slice(kc * P, (kc + 1) * P)
                sp.dma_start(wvr[:, kc, 0:D], a["Wv"][rows, :]).then_inc(s_w, 16)
                sp.dma_start(wvr[:, kc, D:D + E], a["Wr"][rows, :]).then_inc(s_w, 16)
            sp.dma_start(bv[:, :], a["bv"].partition_broadcast(P)).then_inc(s_w, 16)

            def load_x(i, k):
                sp.dma_start(xin[:, k, :, :], x_blocks[i * 2 + k]).then_inc(s_x[k], 16)

            for k in range(2):
                load_x(0, k)
            for q, (w, b) in enumerate((("Wq", "bq"), ("Wk", "bk"))):
                sp.dma_start(wqk[:, q, :, :], a[w].rearrange("(c p) n -> p c n", p=P)).then_inc(s_w, 16)
                sp.dma_start(bqk[:, q, :], a[b]).then_inc(s_qst[q], 16)
            sp.dma_start(cos[:, :], a["c_cos"]).then_inc(s_store[0], 16)
            sp.dma_start(sin[:, :], a["c_sin"]).then_inc(s_store[1], 16)

            def store_block(b, k):
                sp.wait_ge(s_row, 1)
                sp.sem_inc(s_row, -1)
                sp.dma_start(row_blocks[b * 2 + k], row[:, k, :, :]).then_inc(s_store[k], 16)
                for g in range(H // HG):
                    sp.dma_start(v_blocks[b, k, :, :, g, :],
                                 vst[:, k, :, g * HG:(g + 1) * HG, :].rearrange("p t h w -> p t (h w)")).then_inc(s_store[k], 16)

            with sp.Fori(0, NBLK // 2 - 1) as i:
                for k in range(2):
                    store_block(i, k)
                    load_x(i + 1, k)
            for k in range(2):
                store_block(NBLK // 2 - 1, k)

            with sp.Fori(0, B) as b:
                for n in range(S // BLK):
                    for q in range(2):
                        for m in range(KC):
                            r = (n * 2 + q) * KC + m
                            k = r % 2
                            sp.wait_ge(s_q3, b * 8 + (r + 1))
                            for part, tile in enumerate((q1, q2, q3)):
                                for g in range(2):
                                    sp.dma_start(q_blocks[q][part, b, m, n, g],
                                                 tile[g * HG * DH:(g + 1) * HG * DH, k, :]).then_inc(s_qst[k], 16)
            for k in range(2):
                sp.wait_ge(s_store[k], NBLK // 2 * 5 * 16 + 16)
                sp.wait_ge(s_qst[k], B * 4 * 6 * 16 + 16)

        @block.gpsimd
        def _(pool):
            pool.dma_start(bits_i[:, :, :], a["c_bits"].partition_broadcast(P)).then_inc(s_bits, 16)
            pool.memset(ones[:, :], 1.0).then_inc(s_pool, 1)
            pool.iota(tid_i[:, :], [[P, TILES]], 0, channel_multiplier=1).then_inc(s_pool, 1)
            pool.wait_ge(s_pool, 2)
            pool.affine_select(out=upper[:, :], in_=ones[:, :], compare_op=ALU.is_gt, fill=0.0, base=0,
                               pattern=[[1, P]], channel_multiplier=-1).then_inc(s_const, 1)
            pool.tensor_copy(tid[:, :], tid_i[:, :]).then_inc(s_const, 1)
            pool.wait_ge(s_w, 16 * NW)
            pool.wait_ge(s_bits, 16)
            pool.tensor_copy(keep.identb[:, :], keep.ident[:, :]).then_inc(s_const, 1)
            pool.tensor_copy(bits_f[:, :, :], bits_i[:, :, :]).then_inc(s_const, 1)
            pool.memset(thr[:, :], 0).then_inc(s_const, 1)
            pool.wait_ge(s_const, 5)
            pool.wait_ge(s_prob, 2 * NBLK)
            find_threshold(pool, keep, search, 0, FIRST_BITS)

        @block.vector
        def _(dve):
            dve.memset(vst[:, :, :, :, :], 1.0).then_inc(s_one, 1)
            dve.sem_inc(s_v, 1)
            dve.wait_ge(s_one, 1)
            dve.wait_ge(s_const, 5)
            dve.wait_ge(s_w, 16 * NW)

            def statistics(i, k):
                dve.wait_ge(s_x[k], i * 16 + 16)
                for t in range(BT):
                    dve.bn_stats(stats[:, k, t, :], xin[:, k, t, :]).then_inc(s_stat, 1)
                dve.wait_ge(s_stat, BT)
                for t in range(BT):
                    dve.bn_aggr(mean_var[:, k, t, :], stats[:, k, t, :]).then_inc(s_stat, 1)
                dve.wait_ge(s_stat, 2 * BT)
                dve.tensor_scalar(var_eps[:, k, :], mean_var[:, k, :, 1], EPS, None, ALU.add).then_inc(s_var, 1)

            def normalise(i, k, n):
                dve.wait_ge(s_std, n + 1)
                dve.reciprocal(rstd[:, k, :], std[:, k, :]).then_inc(s_stat, 1)
                dve.wait_ge(s_stat, 2 * BT + 1)
                dve.sem_inc(s_stat, -(2 * BT + 1))
                dve.wait_ge(s_store[k], i * 80 + 16)
                for t in range(BT):
                    last = dve.tensor_scalar(row[:, k, t, 0:D], xin[:, k, t, :], mean_var[:, k, t, 0:1],
                                             rstd[:, k, t:t + 1], ALU.subtract, ALU.mult)
                last.then_inc(s_xn, 1)

            def values(n, k):
                dve.wait_ge(s_vr, n + 1)
                dve.tensor_tensor(vst[:, k, :, :, 0:DH], ps[:, 4:4 + BT, 0:D].rearrange("p t (h d) -> p t h d", h=H),
                                  bv[:, :].rearrange("p (h d) -> p h d", h=H).unsqueeze(1).to_broadcast([P, BT, H, DH]), ALU.add)
                dve.tensor_copy(lg[:, k, :, :], ps[:, 4:4 + BT, D:D + E]).then_inc(s_v, 1)
                dve.wait_ge(s_v, n + 2)
                dve.tensor_reduce(lmax[:, k, :], lg[:, k, :, :], AX_X, ALU.max).then_inc(s_soft, 1)
                dve.wait_ge(s_soft, 1)
                dve.tensor_tensor(lsh[:, k, :, :], lg[:, k, :, :],
                                  lmax[:, k, :].unsqueeze(2).to_broadcast([P, BT, E]), ALU.subtract).then_inc(s_sh, 1)

            def probabilities(n, k):
                dve.wait_ge(s_ex, n + 1)
                dve.tensor_reduce(lsum[:, k, :], lexp[:, k, :, :], AX_X, ALU.add).then_inc(s_soft, 1)
                dve.wait_ge(s_soft, 2)
                dve.reciprocal(lrec[:, k, :], lsum[:, k, :]).then_inc(s_soft, 1)
                dve.wait_ge(s_soft, 3)
                dve.sem_inc(s_soft, -3)
                dve.tensor_tensor(row[:, k, :, D:D + E], lexp[:, k, :, :],
                                  lrec[:, k, :].unsqueeze(2).to_broadcast([P, BT, E]), ALU.mult).then_inc(s_prob, 1)
                dve.tensor_tensor(prob[:, bass.ds(n * BT, BT), :], lexp[:, k, :, :],
                                  lrec[:, k, :].unsqueeze(2).to_broadcast([P, BT, E]), ALU.mult).then_inc(s_prob, 1)
                dve.tensor_copy(row[:, k, :, ROW - 1], tid[:, bass.ds(n * BT, BT)]).then_inc(s_row, 1)

            def blocks(i, last):
                for k in range(2):
                    n = i * 2 + k
                    following = (i + k, 1 - k)
                    if not (last and k == 1):
                        statistics(*following)
                    values(n, k)
                    if not (last and k == 1):
                        normalise(*following, n + 1)
                    probabilities(n, k)

            statistics(0, 0)
            normalise(0, 0, 0)
            with dve.Fori(0, NBLK // 2 - 1) as i:
                blocks(i, False)
            blocks(NBLK // 2 - 1, True)

            swap = [j ^ 1 for j in range(32)]
            for k in range(2):
                dve.wait_ge(s_store[k], 16)

            def turn(n, r):
                k = r % 2
                pos = slice(BLK * (r // 4), BLK * (r // 4) + BLK)
                dve.wait_ge(s_qb, n + 3)
                dve.tensor_tensor(qc[:, k, :], qb[:, k, :], cos[:, pos], ALU.mult).then_inc(s_dve, 1)
                dve.stream_shuffle(qsw[:, k, :], qb[:, k, :], swap).then_inc(s_dve, 1)

            def rotate(n, r):
                k = r % 2
                pos = slice(BLK * (r // 4), BLK * (r // 4) + BLK)
                dve.wait_ge(s_dve, n * 3 + 2)
                dve.tensor_tensor(qsn[:, k, :], qsw[:, k, :], sin[:, pos], ALU.mult).then_inc(s_dve, 1)
                dve.wait_ge(s_dve, n * 3 + 3)
                dve.tensor_tensor(qr[:, k, :], qc[:, k, :], qsn[:, k, :], ALU.add).then_inc(s_rope, 1)

            def products(b, last):
                for r in range(8):
                    k = r % 2
                    n = b * 8 + r
                    more = not (last and r == 7)
                    if more:
                        turn(n + 1, (r + 1) % 8)
                    dve.wait_ge(s_q1, n + 1)
                    dve.tensor_tensor(rest[:, k, :], qr[:, k, :], q1[:, k, :], ALU.subtract).then_inc(s_r1, 1)
                    if more:
                        rotate(n + 1, (r + 1) % 8)
                    dve.wait_ge(s_q2, n + 1)
                    dve.tensor_tensor(q3[:, k, :], rest[:, k, :], q2[:, k, :], ALU.subtract).then_inc(s_q3, 1)

            turn(0, 0)
            rotate(0, 0)
            with dve.Fori(0, B - 1) as b:
                products(b, False)
            products(B - 1, True)

        @block.scalar
        def _(act):
            act.sem_inc(s_xnt, 1)
            act.sem_inc(s_qb, 2)
            def copies(n, k):
                act.wait_ge(s_tr, n * 2 + 1)
                act.copy(xt[:, k, 0, :], ps[:, k * 2, :]).then_inc(s_xt, 1)
                act.wait_ge(s_tr, n * 2 + 2)
                act.copy(xt[:, k, 1, :], ps[:, k * 2 + 1, :]).then_inc(s_xt, 1)
                for kc in range(KC):
                    act.copy(xnt[:, kc, bass.ds(n * BLK, BLK)], ps[:, k * 2 + kc, :]).then_inc(s_xnt, 1)

            def blocks(i, last):
                for k in range(2):
                    n = i * 2 + k
                    if not (last and k == 1):
                        act.wait_ge(s_var, n + 2)
                        act.activation(std[:, 1 - k, :], var_eps[:, 1 - k, :], ACT.Sqrt).then_inc(s_std, 1)
                    act.wait_ge(s_sh, n + 1)
                    act.activation(lexp[:, k, :, :], lsh[:, k, :, :], ACT.Exp).then_inc(s_ex, 1)
                    if not (last and k == 1):
                        copies(n + 1, 1 - k)

            act.wait_ge(s_var, 1)
            act.activation(std[:, 0, :], var_eps[:, 0, :], ACT.Sqrt).then_inc(s_std, 1)
            act.wait_ge(s_tr, 1)
            act.copy(xt[:, 0, 0, :], ps[:, 0, :]).then_inc(s_xt, 1)
            act.wait_ge(s_tr, 2)
            act.copy(xt[:, 0, 1, :], ps[:, 1, :]).then_inc(s_xt, 1)
            for kc in range(KC):
                act.copy(xnt[:, kc, 0:BLK], ps[:, kc, :]).then_inc(s_xnt, 1)
            with act.Fori(0, NBLK // 2 - 1) as i:
                blocks(i, False)
            blocks(NBLK // 2 - 1, True)
            for q in range(2):
                act.wait_ge(s_qst[q], 16)

            def biased(n, r):
                k, q, m = r % 2, r // 2 % 2, r % 2
                act.wait_ge(s_pq, n + 1)
                act.activation(qb[:, k, :], ps[:, k, :], ACT.Identity, bias=bqk[:, q, m:m + 1]).then_inc(s_qb, 1)

            def products(b, last):
                for r in range(8):
                    k = r % 2
                    n = b * 8 + r
                    act.wait_ge(s_rope, n + 1)
                    act.wait_ge(s_qst[k], b * 384 + (96 * (r // 2) + 16))
                    act.copy(q1[:, k, :], qr[:, k, :]).then_inc(s_q1, 1)
                    if not (last and r >= 6):
                        biased(n + 2, (r + 2) % 8)
                    act.wait_ge(s_r1, n + 1)
                    act.copy(q2[:, k, :], rest[:, k, :]).then_inc(s_q2, 1)

            for r in range(2):
                biased(r, r)
            with act.Fori(0, B - 1) as b:
                products(b, False)
            products(B - 1, True)

        @block.tensor
        def _(pe):
            pe.wait_ge(s_w, 16 * NW)
            def turn(n, k):
                for kc in range(KC):
                    for t in range(BT):
                        last = pe.transpose(ps[:, k * 2 + kc, t * P:(t + 1) * P],
                                            row[:, k, t, kc * P:(kc + 1) * P], keep.ident[:, :])
                    last.then_inc(s_tr, 1)

            def blocks(i, last):
                for k in range(2):
                    n = i * 2 + k
                    pe.wait_ge(s_xt, n * 2 + 2)
                    pe.wait_ge(s_v, n + 1)
                    for t in range(BT):
                        for kc in range(KC):
                            done = pe.matmul(ps[:, 4 + t, 0:D + E], xt[:, k, kc, t * P:(t + 1) * P],
                                             wvr[:, kc, :], start=(kc == 0), stop=(kc == KC - 1))
                    done.then_inc(s_vr, 1)
                    if not (last and k == 1):
                        pe.wait_ge(s_xn, n + 2)
                        pe.wait_ge(s_xnt, n * KC + 1)
                        turn(n + 1, 1 - k)

            pe.wait_ge(s_xn, 1)
            turn(0, 0)
            with pe.Fori(0, NBLK // 2 - 1) as i:
                blocks(i, False)
            blocks(NBLK // 2 - 1, True)
            with pe.Fori(0, B) as b:
                pe.wait_ge(s_xnt, KC * NBLK + 1)
                for r in range(8):
                    k, blk, q, m = r % 2, r // 4, r // 2 % 2, r % 2
                    pe.wait_ge(s_qb, b * 8 + (r + 1))
                    for kc in range(KC):
                        last = pe.matmul(ps[:, k, :], wqk[:, q, kc, m * P:(m + 1) * P],
                                         xnt[:, kc, bass.ds(b * S + blk * BLK, BLK)],
                                         start=(kc == 0), stop=(kc == KC - 1))
                    last.then_inc(s_pq, 1)


def attention_stage(nc, ctx, keep, xrow, slots_dram, qs_dram, ks_dram, v_dram):
    def sb(name, shape, dt=F32):
        return ctx.enter_context(nc.sbuf_tensor(name, shape, dt))

    def sem(name):
        return ctx.enter_context(nc.semaphore(name))

    ps = keep.psum
    SB, TB, OB = 0, 4, 6
    qst = sb("qst", [P, 2, 2, HG, HALF], BF16)
    kst = sb("kst", [P, 2, 2, HG, HALF], BF16)
    vgr = sb("vgr", [P, 2, QT, HG * VW])
    pt = sb("pt", [P, 2, HG, HALF])
    mx = sb("mx", [P, 2, HG, QT // 2])
    negm = sb("negm", [P, 2, 2 * MROWS, HG, QT // 2], BF16)
    mrest = sb("mrest", [P, 2, HG, QT // 2])
    mrow = sb("mrow", [MROWS * HG * QT // 2, 2, P], BF16)
    osb = sb("osb", [P, 2, HALF])
    den = sb("den", [P, 2, QT // 2, HG])
    stage = sb("stage", [P, 2, ROW])
    where = sb("where", [P, 2, E], U32)

    prob, thr, tot = keep.prob, keep.thr, keep.tot
    diff = sb("a_diff", [P, TILES, E])
    mask = sb("mask", [P, 2, TILES, E], BF16)
    inside = sb("inside", [P, 2, TILES, E])
    off0 = sb("off0", [P, 2, TILES, E])
    off1 = sb("off1", [P, 2, TILES, E])
    rank = sb("rank", [P, 2, TILES, E])
    fits = sb("fits", [P, TILES, E])
    slot_f = sb("slot_f", [P, TILES, E])
    slot_t = sb("slot_t", [P, TILES, E])

    search = Search(ctx, nc, "late_")

    s_slot = sem("s_slot")
    s_mask = sem("s_mask")
    s_pre = sem("s_pre")
    s_ins = sem("s_ins")
    in_stack = [sem("in_stack0"), sem("in_stack1")]
    s_const = sem("a_const")
    st_ready = sem("st_ready")
    exp_done = sem("exp_done")
    pv_done = sem("pv_done")
    s_ready = sem("s_ready")
    max_done = sem("max_done")
    split = sem("split")
    neg_ready = sem("neg_ready")
    neg_t = sem("neg_t")
    mrow_ready = sem("mrow_ready")
    mrow_in = [sem("mrow_in0"), sem("mrow_in1")]
    o_copied = sem("o_copied")
    o_t = sem("o_t")
    o_rec = sem("o_rec")
    o_norm = sem("o_norm")
    in_row = [sem("in_row0"), sem("in_row1")]
    s_freed = sem("s_freed")
    s_where = sem("s_where")
    sent = [sem("sent0"), sem("sent1")]
    UNITS = 2 * QT
    LAG = 4
    NLOAD = 2 * len(TERMS) + 1
    TURN_A, TURN_B = 12, 4

    with nc.Block() as block:
        @block.sync
        def _(sp):
            def load_stack(g, par):
                for r, (pq, pk) in enumerate(TERMS):
                    rows = slice(r * DH, (r + 1) * DH)
                    sp.dma_start(qst[rows, par, :, :, :].rearrange("r h j s -> r (h j) s"),
                                 qs_dram[pq, g].rearrange("q r s -> r q s")).then_inc(in_stack[par], 16)
                    sp.dma_start(kst[rows, par, :, :, :].rearrange("r h j s -> r (h j) s"),
                                 ks_dram[pk, g].rearrange("q r s -> r q s")).then_inc(in_stack[par], 16)
                sp.dma_start(vgr[:, par, :, :], v_dram[g]).then_inc(in_stack[par], 16)

            def put_max(g, par, half):
                sp.wait_ge(mrow_ready, g * 2 + (half + 1))
                n = HG * QT // 2
                for part in range(MROWS):
                    sp.dma_start(qst[SROWS + part:SROWS + part + 1, par, half, :, :].rearrange("o j (q t) -> o (j q) t", t=P),
                                 mrow[part * n:(part + 1) * n, half, :]).then_inc(mrow_in[half], 16)

            load_stack(0, 0)
            load_stack(1, 1)
            put_max(0, 0, 0)
            put_max(0, 0, 1)

            def group(g, par):
                put_max(g + 1, 1 - par, 0)
                sp.wait_ge(pv_done, g * UNITS + UNITS)
                load_stack(g + 2, par)
                put_max(g + 1, 1 - par, 1)

            with sp.Fori(0, (GROUPS - 2) // 2) as i:
                for par in range(2):
                    group(i * 2 + par, par)
            put_max(GROUPS - 1, 1, 0)
            put_max(GROUPS - 1, 1, 1)

        @block.gpsimd
        def _(pool):
            rows = xrow.rearrange("(t p) c -> t p c", p=P)

            def load(t, par):
                pool.dma_start(stage[:, par, :], rows[t]).then_inc(in_row[par], 16)

            load(0, 0)
            load(1, 1)
            done = [0]

            def chain(instruction):
                done[0] += 1
                instruction.then_inc(s_slot, 1)
                pool.wait_ge(s_slot, done[0])

            find_threshold(pool, keep, search, FIRST_BITS, BITS)
            chain(pool.tensor_tensor(diff[:, :, :], prob[:, :, :],
                                     thr[:, :].bitcast(F32).unsqueeze(1).to_broadcast([P, TILES, E]), ALU.subtract))
            pool.tensor_scalar(mask[:, 0, :, :], diff[:, :, :], 0.0, None, ALU.is_gt).then_inc(s_mask, 1)
            pool.tensor_scalar(mask[:, 1, :, :], diff[:, :, :], 0.0, None, ALU.is_equal).then_inc(s_mask, 1)
            pool.wait_ge(s_ins, 4)
            src, dst = off0, off1
            for shift in (1, 2, 4, 8, 16):
                chain(pool.tensor_copy(dst[:, :, 0:shift, :], src[:, :, 0:shift, :]))
                chain(pool.tensor_tensor(dst[:, :, shift:TILES, :], src[:, :, shift:TILES, :],
                                         src[:, :, 0:TILES - shift, :], ALU.add))
                src, dst = dst, src
            chain(pool.tensor_tensor(rank[:, :, :, :], src[:, :, :, :], inside[:, :, :, :], ALU.add))
            above = dst
            chain(pool.tensor_tensor(above[:, 0, 0, :], rank[:, 0, TILES - 1, :], mask[:, 0, TILES - 1, :], ALU.add))
            chain(pool.affine_select(out=above[:, 0, 1, :], in_=above[:, 0, 0, :], compare_op=ALU.is_ge, fill=0.0,
                                     base=-(P - 1), pattern=[[0, E]], channel_multiplier=1))
            chain(pool.partition_all_reduce(tot[:, :], above[:, 0, 1, :], P, RADD))
            chain(pool.tensor_tensor(rank[:, 1, :, :], rank[:, 1, :, :],
                                     tot[:, :].unsqueeze(1).to_broadcast([P, TILES, E]), ALU.add))
            chain(pool.tensor_scalar(fits[:, :, :], rank[:, 1, :, :], float(CAP), None, ALU.is_lt))
            chain(pool.tensor_tensor(fits[:, :, :], fits[:, :, :], mask[:, 1, :, :], ALU.mult))
            for e in range(E):
                chain(pool.tensor_scalar(rank[:, :, :, e], rank[:, :, :, e], float(CAP * e) - NOWHERE, None, ALU.add))
            chain(pool.tensor_tensor(slot_f[:, :, :], rank[:, 0, :, :], mask[:, 0, :, :], ALU.mult))
            chain(pool.tensor_tensor(slot_t[:, :, :], rank[:, 1, :, :], fits[:, :, :], ALU.mult))
            chain(pool.tensor_tensor(slot_f[:, :, :], slot_f[:, :, :], slot_t[:, :, :], ALU.add))
            chain(pool.tensor_scalar(keep.slot[:, :, :], slot_f[:, :, :], NOWHERE, None, ALU.add))

            def scatter(i, par):
                pool.tensor_copy(where[:, par, :], keep.slot[:, bass.ds(i * 2 + par, 1), :].rearrange("p o e -> p (o e)"))\
                    .then_inc(s_where, 1)
                pool.wait_ge(s_where, 1)
                pool.wait_ge(in_row[par], i * 16 + 16)
                pool.sem_inc(s_where, -1)
                for e in range(E):
                    pool.indirect_dma_start(
                        out=slots_dram[:, :], out_offset=bass.IndirectOffsetOnAxis(ap=where[:, par, e:e + 1], axis=0),
                        in_=stage[:, par, :], in_offset=None, bounds_check=E * CAP - 1, oob_is_err=False,
                    ).then_inc(sent[par], 16)

            with pool.Fori(0, TILES // 2 - 1) as i:
                for par in range(2):
                    scatter(i, par)
                for par in range(2):
                    pool.wait_ge(sent[par], i * (16 * E) + 16 * E)
                    pool.sem_inc(s_freed, 1)
                    load(i * 2 + (par + 2), par)
            for par in range(2):
                scatter(TILES // 2 - 1, par)
            for par in range(2):
                pool.wait_ge(sent[par], TILES // 2 * E * 16)

        @block.tensor
        def _(pe):
            def scores_t(g, par, u, half_turn):
                half, kt = u // QT, u % QT
                for j in range(HG):
                    n = g * (UNITS * HG) + (u * HG + j)
                    if j == 0 and u % QT == 0:
                        pe.wait_ge(mrow_in[half], g * (16 * MROWS) + 16 * MROWS)
                    if not (isinstance(g, int) and n < 2):
                        pe.wait_ge(exp_done, n - 1)
                    pe.matmul(ps[:, TB + j % 2, :], kst[0:SROWS + MROWS, par, kt // 4, j, kt % 4 * P:(kt % 4 + 1) * P],
                              qst[0:SROWS + MROWS, par, half, j, :],
                              start=True, stop=True).then_inc(st_ready, 1)
                    yield

            def scores(g, par, s):
                qt, j = s // HG, s % HG
                n = g * (QT * HG) + s
                if not (isinstance(g, int) and n < 2):
                    pe.wait_ge(max_done, n - 1)
                for half in range(2):
                    last = pe.matmul(ps[:, SB + 2 * (s % 2) + half, :], qst[0:SROWS, par, qt // 4, j, qt % 4 * P:(qt % 4 + 1) * P],
                                     kst[0:SROWS, par, half, j, :], start=True, stop=True)
                last.then_inc(s_ready, 1)

            def outputs(g, par, u):
                half, kt = u // QT, u % QT
                if kt == 0:
                    pe.wait_ge(mrow_ready, g * 2 + (half + 1))
                pe.wait_ge(exp_done, g * (UNITS * HG) + (u + 1) * HG)
                for j in range(HG):
                    last = pe.matmul(ps[VW * j:VW * (j + 1), OB + half, :], vgr[:, par, kt, VW * j:VW * (j + 1)],
                                     pt[:, u % 2, j, :], start=(kt == 0), stop=(kt == QT - 1))
                last.then_inc(pv_done, 1)

            def turn_max(g, half):
                n = MROWS * HG * QT // 2
                pe.wait_ge(neg_ready, g * 2 + (half + 1))
                pe.transpose(ps[0:2 * n, OB + half, 0:P // 2].bitcast(BF16),
                             negm[:, half, :, :, :].rearrange("p a j q -> p (a j q)"), keep.identb[:, :]).then_inc(neg_t, 1)

            def turn_outputs(g, half):
                pe.wait_ge(o_copied, g * 2 + (half + 1))
                for t in range(QT // 2):
                    last = pe.transpose(ps[:, OB + half, t * P:(t + 1) * P], osb[:, half, t * P:(t + 1) * P],
                                        keep.ident[:, :])
                last.then_inc(o_t, 1)

            def count(weights):
                flat_mask = mask[:, :, :, :].rearrange("p m t e -> p (m t e)")
                pe.matmul(ps[:, OB, :], weights[:, :], flat_mask, start=True, stop=True).then_inc(s_pre, 1)

            pe.wait_ge(s_const, 2)
            pe.wait_ge(in_stack[0], 16 * NLOAD)
            for s in range(QT * HG):
                scores(0, 0, s)
            turn_max(0, 0)
            for _ in scores_t(0, 0, 0, 0):
                pass

            def tiles_of_scores(g, par, u, first, last):
                if u >= LAG and not last:
                    return [(g + 1, 1 - par, 2 * (u - LAG) + n) for n in range(2)]
                if u < LAG and not first:
                    return [(g, par, 2 * (u + UNITS - LAG) + n) for n in range(2)]
                return []

            def group(g, par, turns, first, last):
                for u in range(UNITS):
                    tiles = tiles_of_scores(g, par, u, first, last)
                    if u == LAG and not last:
                        pe.wait_ge(in_stack[1 - par], turns * (16 * NLOAD) + 16 * NLOAD)
                    if u + 1 < UNITS:
                        ahead = scores_t(g, par, u + 1, 0)
                    else:
                        ahead = scores_t(g + 1, 1 - par, 0, 0) if not last else iter(())
                    next(ahead, None)
                    for tile in tiles:
                        scores(*tile)
                    next(ahead, None)
                    next(ahead, None)
                    outputs(g, par, u)
                    for _ in ahead:
                        pass
                    if u == 2 and not first:
                        turn_outputs(g - 1, 1)
                    if u == TURN_B:
                        if not first:
                            pe.wait_ge(o_norm, g * 2)
                        turn_max(g, 1)
                    if u == QT + 2:
                        turn_outputs(g, 0)
                    if u == TURN_A and not last:
                        pe.wait_ge(o_norm, g * 2 + 1)
                        turn_max(g + 1, 0)
                    if first and u == UNITS - 2:
                        pe.wait_ge(mrow_ready, 3)
                        pe.wait_ge(s_mask, 2)
                        count(keep.upper)
                    if first and u == UNITS - 1:
                        pe.wait_ge(s_ins, 2)
                        count(keep.ones)

            group(0, 0, 0, True, False)
            pe.wait_ge(s_ins, 4)
            with pe.Fori(0, (GROUPS - 2) // 2) as i:
                group(i * 2 + 1, 1, i + 1, False, False)
                group(i * 2 + 2, 0, i + 1, False, False)
            group(GROUPS - 1, 1, None, False, True)
            turn_outputs(GROUPS - 1, 1)

        @block.scalar
        def _(act):
            def rows_of_max(g, half):
                n = MROWS * HG * QT // 2
                act.wait_ge(neg_t, g * 2 + (half + 1))
                if not (isinstance(g, int) and g == 0):
                    act.wait_ge(mrow_in[half], g * (16 * MROWS))
                act.copy(mrow[:, half, :], ps[0:n, OB + half, 0:P // 2].bitcast(BF16)).then_inc(mrow_ready, 1)

            def copy_outputs(g, half):
                act.wait_ge(pv_done, g * UNITS + (half + 1) * QT)
                if not (isinstance(g, int) and g == 0):
                    act.wait_ge(o_t, g * 2 + (half - 1))
                act.copy(osb[:, half, :], ps[:, OB + half, :]).then_inc(o_copied, 1)

            def group(g, first, last):
                for u in range(UNITS):
                    if not (first and u < 2):
                        act.wait_ge(pv_done, g * UNITS + (u - 1))
                    for j in range(HG):
                        act.wait_ge(st_ready, g * (UNITS * HG) + (u * HG + j + 1))
                        act.activation(pt[:, u % 2, j, :], ps[:, TB + j % 2, :], ACT.Exp, scale=SCALE).then_inc(exp_done, 1)
                    if u == 1 and not first:
                        copy_outputs(g - 1, 1)
                    if u == TURN_B + 1:
                        rows_of_max(g, 1)
                    if u == QT + 1:
                        copy_outputs(g, 0)
                    if u == TURN_A + 1 and not last:
                        rows_of_max(g + 1, 0)

            rows_of_max(0, 0)
            group(0, True, False)
            with act.Fori(0, GROUPS - 2) as i:
                group(i + 1, False, False)
            group(GROUPS - 1, False, True)
            copy_outputs(GROUPS - 1, 1)

        @block.vector
        def _(dve):
            dve.memset(kst[SROWS:P, :, :, :, :], 1.0).then_inc(s_const, 1)
            dve.memset(negm[:, :, :, :, :], 0.0).then_inc(s_const, 1)
            dve.memset(off0[:, :, 0, :], 0.0).then_inc(s_ins, 1)
            dve.wait_ge(s_const, 2)

            def take_max(g, s):
                qt, j = s // HG, s % HG
                dve.wait_ge(s_ready, g * (QT * HG) + (s + 1))
                dve.tensor_reduce(mx[:, qt // 4, j, qt % 4:qt % 4 + 1], ps[:, SB + 2 * (s % 2):SB + 2 * (s % 2) + 2, :]
                                  .rearrange("p b n -> p (b n)"), AX_X, ALU.max).then_inc(max_done, 1)

            def split_max(g, half):
                m = mx[:, half, :, :]
                dve.wait_ge(max_done, g * (QT * HG) + (half + 1) * (QT * HG // 2))
                if not (isinstance(g, int) and g == 0):
                    dve.wait_ge(neg_t, g * 2 + (half - 1))
                at = g * 6 + 3 * half
                dve.tensor_scalar(negm[:, half, 0, :, :], m, -1.0, None, ALU.mult).then_inc(split, 1)
                dve.wait_ge(split, at + 1)
                dve.scalar_tensor_tensor(out=mrest[:, half, :, :], in0=m, scalar=-1.0, in1=negm[:, half, 0, :, :],
                                         op0=ALU.mult, op1=ALU.subtract).then_inc(split, 1)
                dve.wait_ge(split, at + 2)
                dve.tensor_copy(negm[:, half, 1, :, :], mrest[:, half, :, :]).then_inc(split, 1)
                dve.wait_ge(split, at + 3)
                dve.tensor_tensor(negm[:, half, 2, :, :], mrest[:, half, :, :], negm[:, half, 1, :, :],
                                  ALU.subtract).then_inc(neg_ready, 1)

            def normalise(pair, par, half):
                g = pair * 2 + par
                o = ps[:, OB + half, :].rearrange("p (t j w) -> p t j w", t=QT // 2, j=HG)
                dve.wait_ge(o_t, g * 2 + (half + 1))
                dve.reciprocal(den[:, half, :, :], o[:, :, :, DH]).then_inc(o_rec, 1)
                dve.wait_ge(o_rec, g * 2 + (half + 1))
                where_to = keep.heads[:, bass.ds(pair, 1), half * (QT // 2):(half + 1) * (QT // 2),
                                      par * HG * DH:(par + 1) * HG * DH]
                dve.tensor_tensor(where_to.rearrange("p o t (j d) -> p (o t) j d", j=HG), o[:, :, :, 0:DH],
                                  den[:, half, :, :].unsqueeze(3).to_broadcast([P, QT // 2, HG, DH]),
                                  ALU.mult).then_inc(o_norm, 1)

            for s in range(QT * HG):
                take_max(0, s)
                if s % 16 == 15:
                    split_max(0, s // 16)

            def group(pair, par, first, last):
                g = pair * 2 + par
                for u in range(UNITS):
                    for n in range(2):
                        if u >= LAG and not last:
                            take_max(g + 1, 2 * (u - LAG) + n)
                        if u < LAG and not first:
                            take_max(g, 2 * (u + UNITS - LAG) + n)
                    if u == LAG + QT - 1 and not last:
                        split_max(g + 1, 0)
                    if u == LAG - 1 and not first:
                        split_max(g, 1)
                    if u == 2 and not first:
                        normalise(pair - (1 - par), 1 - par, 1)
                    if u == QT + 2:
                        normalise(pair, par, 0)
                    if first and u == UNITS - 1:
                        counts = ps[:, OB, :].rearrange("p (m t e) -> p m t e", m=2, t=TILES)
                        dve.wait_ge(s_pre, 1)
                        dve.tensor_copy(inside[:, :, :, :], counts).then_inc(s_ins, 1)
                        dve.wait_ge(s_pre, 2)
                        for m in range(2):
                            dve.tensor_copy(off0[:, m, 1:TILES, :], counts[:, m, 0:TILES - 1, :]).then_inc(s_ins, 1)

            group(0, 0, True, False)
            with dve.Fori(0, (GROUPS - 2) // 2) as i:
                group(i, 1, False, False)
                group(i + 1, 0, False, False)
            group(GROUPS // 2 - 1, 1, False, True)
            normalise(GROUPS // 2 - 1, 1, 1)


def project_stage(nc, ctx, a, keep, out):
    def sb(name, shape, dt=F32):
        return ctx.enter_context(nc.sbuf_tensor(name, shape, dt))

    def sem(name):
        return ctx.enter_context(nc.semaphore(name))

    ps = keep.psum
    PB = 4
    xres = sb("xres", [P, 2, PB, D])
    base = sb("base", [P, 2, PB, D])
    fin = sb("fin", [P, 2, PB, D])
    turn = sb("turn", [P, 2, KC, P])
    ht = sb("ht", [P, 2, KC, P])
    in_x = [sem("p_x0"), sem("p_x1")]
    s_turn = sem("p_turn")
    s_ht = sem("p_turned")
    s_hc = sem("p_copied")
    s_y = sem("p_product")
    s_base = sem("p_base")
    s_fin = sem("p_final")
    s_seen = sem("p_seen")
    stored = [sem("p_stored0"), sem("p_stored1")]
    x_blocks = a["x"].rearrange("b (h t p) d -> (b h) p t d", p=P, t=PB)
    out_blocks = out.rearrange("b (h t p) d -> (b h) p t d", p=P, t=PB)

    with nc.Block() as block:
        @block.sync
        def _(sp):
            sp.dma_start(keep.wo[:, :, :], a["Wo"].rearrange("(c p) n -> p c n", p=P)).then_inc(stored[0], 16)
            sp.dma_start(keep.bo[:, :], a["bo"].partition_broadcast(P)).then_inc(stored[1], 16)
            for h in range(2):
                sp.dma_start(xres[:, h, :, :], x_blocks[h]).then_inc(in_x[h], 16)

            def store(b, h):
                sp.wait_ge(s_fin, b * QT + (PB * (h + 1) + 2))
                sp.dma_start(out_blocks[b * 2 + h], fin[:, h, :, :]).then_inc(stored[h], 16)

            with sp.Fori(0, B - 1) as b:
                for h in range(2):
                    store(b, h)
                    sp.dma_start(xres[:, h, :, :], x_blocks[b * 2 + (h + 2)]).then_inc(in_x[h], 16)
            for h in range(2):
                store(B - 1, h)
            for h in range(2):
                sp.wait_ge(stored[h], B * 16 + 16)

        @block.gpsimd
        def _(pool):
            with pool.Fori(0, B) as b:
                for q in range(QT):
                    pool.wait_ge(s_ht, b * QT + (q + 1))
                    pool.sem_inc(s_seen, 1)
                    pool.tensor_copy(turn[:, q % 2, :, :],
                                     keep.heads[:, bass.ds(b * KC, KC), q, :]).then_inc(s_turn, 1)

        @block.tensor
        def _(pe):
            def turn_tile(b, q):
                pe.wait_ge(s_turn, b * QT + (q + 1))
                pe.wait_ge(s_hc, b * QT + (q + 1))
                for kc in range(KC):
                    last = pe.transpose(ps[:, q % 2, kc * P:(kc + 1) * P], turn[:, q % 2, kc, :], keep.ident[:, :])
                last.then_inc(s_ht, 1)

            def product(b, q):
                k = q % 2
                pe.wait_ge(s_hc, b * QT + (q + 3))
                pe.wait_ge(s_fin, b * QT + (q + 1))
                for kc in range(KC):
                    last = pe.matmul(ps[:, 2 + k, 0:D], ht[:, k, kc, :], keep.wo[:, kc, :],
                                     start=(kc == 0), stop=(kc == KC - 1))
                last.then_inc(s_y, 1)

            pe.sem_inc(s_ht, 2)
            pe.sem_inc(s_y, 2)
            pe.wait_ge(stored[0], 16)
            turn_tile(0, 0)
            with pe.Fori(0, B - 1) as b:
                for q in range(QT):
                    turn_tile(b, q + 1)
                    product(b, q)
            for q in range(QT):
                if q < QT - 1:
                    turn_tile(B - 1, q + 1)
                product(B - 1, q)

        @block.scalar
        def _(act):
            act.sem_inc(s_hc, 2)
            with act.Fori(0, B) as b:
                for q in range(QT):
                    k = q % 2
                    act.wait_ge(s_ht, b * QT + (q + 3))
                    act.wait_ge(s_y, b * QT + (q + 1))
                    act.copy(ht[:, k, :, :].rearrange("p c n -> p (c n)"), ps[:, k, 0:KC * P]).then_inc(s_hc, 1)

        @block.vector
        def _(dve):
            dve.sem_inc(s_fin, 2)
            dve.wait_ge(stored[1], 16)
            with dve.Fori(0, B) as b:
                for h in range(2):
                    dve.wait_ge(in_x[h], b * 16 + 16)
                    dve.tensor_tensor(base[:, h, :, :], xres[:, h, :, :],
                                      keep.bo[:, :].unsqueeze(1).to_broadcast([P, PB, D]), ALU.add).then_inc(s_base, 1)
                    dve.wait_ge(s_base, b * 2 + (h + 1))
                    dve.wait_ge(stored[h], b * 16 + 16)
                    for t in range(PB):
                        q = h * PB + t
                        dve.wait_ge(s_y, b * QT + (q + 3))
                        dve.tensor_tensor(fin[:, h, t, :], ps[:, 2 + q % 2, 0:D], base[:, h, t, :], ALU.add).then_inc(s_fin, 1)


def expert_stage(nc, ctx, a, keep, slots_dram, out):
    def sb(name, shape, dt=F32):
        return ctx.enter_context(nc.sbuf_tensor(name, shape, dt))

    def sem(name):
        return ctx.enter_context(nc.semaphore(name))

    ps = keep.psum
    w1 = sb("w1", [P, KC, DI])
    w1h = sb("w1_high", [P, KC, DI], F32R)
    w1l = sb("w1_low", [P, KC, DI], F32R)
    w2 = sb("w2", [P, FC, D])
    w2h = sb("w2_high", [P, FC, D], F32R)
    w2l = sb("w2_low", [P, FC, D], F32R)
    b1 = sb("b1", [P, 2, FC])
    b2 = sb("b2", [P, 2, D])
    rows = sb("rows", [P, 2, ST, ROW])
    xh = sb("x_high", [P, KC, CAP], F32R)
    xl = sb("x_low", [P, KC, CAP], F32R)
    hidden = sb("hidden", [P, 2, CAP])
    hh = sb("h_high", [P, FC, CAP], F32R)
    hl = sb("h_low", [P, FC, CAP], F32R)
    ids = sb("ids", [P, 2, ST], U32)
    gain = sb("e_gain", [P, 2, ST])
    ysum = sb("ysum", [P, 2, D])
    yout = sb("yout", [P, ST, D])
    in_w1 = sem("e_in_w1")
    in_w2 = sem("e_in_w2")
    in_rows = [sem("e_in_rows0"), sem("e_in_rows1")]
    w1h_ready = sem("e_w1_high")
    w1l_ready = sem("e_w1_low")
    w2h_ready = sem("e_w2_high")
    w2l_ready = sem("e_w2_low")
    turned = sem("e_turned")
    x_high = sem("e_x_high")
    x_in = sem("e_x_in")
    h_ready = sem("e_h_ready")
    h_in = sem("e_h_in")
    h_high = sem("e_h_high")
    h_parts = sem("e_h_parts")
    y_ready = sem("e_y_ready")
    y_sum = sem("e_y_sum")
    y_out = sem("e_y_out")
    s_ids = sem("e_ids")
    s_seen = sem("e_seen")
    added = sem("e_added")
    adds_done = sem("e_adds_done")
    NL = 3
    TURN = (6, 7, 0, 1)
    out_rows = out.rearrange("b s d -> (b s) d")
    slot_rows = slots_dram.rearrange("(e t p) c -> e p t c", e=E, p=P)
    w1_dram = a["W1"].rearrange("e (c p) n -> e p c n", p=P)
    w2_dram = a["W2"].rearrange("e (c p) n -> e p c n", p=P)

    with nc.Block() as block:
        def experts(engine, expert):
            with engine.Fori(0, E // 2 - 1) as i:
                for k in range(2):
                    expert(i * 2 + k, k, False)
            for k in range(2):
                expert(E - 2 + k, k, k == 1)

        @block.sync
        def _(sp):
            def load_rows(e, k):
                sp.dma_start(rows[:, k, :, :], slot_rows[e]).then_inc(in_rows[k], 16)
                sp.dma_start(b1[:, k, :], a["b1"][e]).then_inc(in_rows[k], 16)
                sp.dma_start(b2[:, k, :], a["b2"][e].partition_broadcast(P)).then_inc(in_rows[k], 16)

            sp.dma_start(w1[:, :, :], w1_dram[0]).then_inc(in_w1, 16)
            load_rows(0, 0)
            sp.dma_start(w2[:, :, :], w2_dram[0]).then_inc(in_w2, 16)
            load_rows(1, 1)

            def weights(e):
                sp.wait_ge(w1l_ready, e)
                sp.dma_start(w1[:, :, :], w1_dram[e]).then_inc(in_w1, 16)
                sp.wait_ge(w2l_ready, e)
                sp.dma_start(w2[:, :, :], w2_dram[e]).then_inc(in_w2, 16)

            with sp.Fori(0, E // 2 - 1) as i:
                for k in range(2):
                    weights(i * 2 + (k + 1))
                    sp.wait_ge(y_out, i * (2 * ST) + (k + 1) * ST)
                    load_rows(i * 2 + (k + 2), k)
            weights(E - 1)

        @block.gpsimd
        def _(pool):
            def low(part, whole, high, ready):
                pool.tensor_tensor(part, whole, high.bitcast(F32), ALU.subtract).then_inc(ready, 1)

            pool.sem_inc(adds_done, 1)
            pool.wait_ge(w1h_ready, 1)
            low(w1l[:, :, :], w1[:, :, :], w1h[:, :, :], w1l_ready)

            def expert(e, k, last):
                pool.wait_ge(w2h_ready, e + 1)
                low(w2l[:, :, :], w2[:, :, :], w2h[:, :, :], w2l_ready)
                if not last:
                    pool.wait_ge(w1h_ready, e + 2)
                    low(w1l[:, :, :], w1[:, :, :], w1h[:, :, :], w1l_ready)
                pool.wait_ge(s_ids, e + 1)
                pool.sem_inc(s_seen, 1)
                for t in range(ST):
                    pool.wait_ge(y_out, e * ST + (t + 1))
                    pool.sem_inc(s_seen, 1)
                    pool.indirect_dma_start(
                        out=out_rows, out_offset=bass.IndirectOffsetOnAxis(ap=ids[:, k, t:t + 1], axis=0),
                        in_=yout[:, t, :], in_offset=None, bounds_check=TOK - 1, compute_op=ALU.add,
                    ).then_inc(added, 16)
                pool.wait_ge(added, e * (16 * ST) + 16 * ST)
                pool.sem_inc(adds_done, 1)

            experts(pool, expert)

        @block.tensor
        def _(pe):
            def turn_rows(e, k, first):
                pe.wait_ge(in_rows[k], 16 * NL if first else (e - k) * (8 * NL) + 16 * NL)
                for b in range(4):
                    kc, half = b // 2, b % 2
                    if b < 2 and not first:
                        pe.wait_ge(x_in, e * 4 + (b - 1))
                    elif b == 2 and not first:
                        pe.wait_ge(h_in, e * FC + 1)
                    for t in range(4):
                        last = pe.transpose(ps[:, TURN[b], t * P:(t + 1) * P],
                                            rows[:, k, half * 4 + t, kc * P:(kc + 1) * P], keep.ident[:, :])
                    last.then_inc(turned, 1)

            pe.sem_inc(y_ready, 1)
            turn_rows(0, 0, True)

            def expert(e, k, last):
                pe.wait_ge(w1l_ready, e + 1)
                pe.wait_ge(x_in, e * 4 + 4)
                for f in range(FC):
                    pe.wait_ge(h_in, e * FC + (f + 1))
                    chunk = slice(f * P, (f + 1) * P)
                    parts = [(w, x, kc) for w, x in ((w1h, xh), (w1h, xl), (w1l, xh)) for kc in range(KC)]
                    for n, (w, x, kc) in enumerate(parts):
                        for half in range(2):
                            done = pe.matmul(ps[:, 2 * (f % 2) + half, :], w[:, kc, chunk],
                                             x[:, kc, half * 512:(half + 1) * 512],
                                             start=(n == 0), stop=(n == len(parts) - 1))
                    done.then_inc(h_ready, 1)
                if not last:
                    turn_rows(e + 1, 1 - k, False)
                pe.wait_ge(w2l_ready, e + 1)

                def outputs(t, chunks):
                    slots = slice(t * P, (t + 1) * P)
                    for f in chunks:
                        if t == 0:
                            pe.wait_ge(h_parts, e * FC + (f + 3))
                        for n, (h, w) in enumerate(((hh, w2h), (hh, w2l), (hl, w2h))):
                            done = pe.matmul(ps[:, 4 + t % 2, 0:D], h[:, f, slots], w[:, f, :],
                                             start=(f == 0 and n == 0), stop=(f == FC - 1 and n == 2))
                    if FC - 1 in chunks:
                        done.then_inc(y_ready, 1)

                for chunks in (range(FC - 1), range(FC - 1, FC)):
                    for t in range(2):
                        if 0 in chunks:
                            pe.wait_ge(y_sum, e * ST + (t + 1))
                        outputs(t, chunks)
                for t in range(2, ST):
                    pe.wait_ge(y_sum, e * ST + (t + 1))
                    outputs(t, range(FC))

            experts(pe, expert)

        @block.scalar
        def _(act):
            act.sem_inc(h_in, 2)
            act.wait_ge(in_w1, 16)
            act.copy(w1h[:, :, :], w1[:, :, :]).then_inc(w1h_ready, 1)

            def expert(e, k, last):
                act.wait_ge(y_ready, e * ST + 1)
                act.wait_ge(in_w2, e * 16 + 16)
                act.copy(w2h[:, :, :], w2[:, :, :]).then_inc(w2h_ready, 1)
                for f in range(FC):
                    act.wait_ge(h_ready, e * FC + (f + 1))
                    act.wait_ge(h_parts, e * FC + (f + 1))
                    act.activation(hidden[:, f % 2, :].rearrange("p (b n) -> p b n", b=2),
                                   ps[:, 2 * (f % 2):2 * (f % 2) + 2, :],
                                   ACT.Gelu, bias=b1[:, k, f:f + 1]).then_inc(h_in, 1)
                if not last:
                    act.wait_ge(in_w1, e * 16 + 32)
                    act.copy(w1h[:, :, :], w1[:, :, :]).then_inc(w1h_ready, 1)

            experts(act, expert)

        @block.vector
        def _(dve):
            def split_rows(e, first):
                for b in range(4):
                    kc, half = b // 2, b % 2
                    at = slice(half * 512, (half + 1) * 512)
                    dve.wait_ge(turned, b + 1 if first else e * 4 + (b + 1))
                    dve.tensor_copy(xh[:, kc, at], ps[:, TURN[b], :]).then_inc(x_high, 1)
                    dve.wait_ge(x_high, b + 1 if first else e * 4 + (b + 1))
                    dve.tensor_tensor(xl[:, kc, at], ps[:, TURN[b], :], xh[:, kc, at].bitcast(F32),
                                      ALU.subtract).then_inc(x_in, 1)

            dve.sem_inc(y_sum, 2)
            dve.sem_inc(h_parts, 2)
            split_rows(0, True)

            def expert(e, k, last):
                dve.wait_ge(in_rows[k], (e - k) * (8 * NL) + 16 * NL)
                dve.tensor_copy(gain[:, k, :], rows[:, k, :, bass.ds(e + D, 1)].rearrange("p t o -> p (t o)"))
                dve.tensor_copy(ids[:, k, :], rows[:, k, :, ROW - 1]).then_inc(s_ids, 1)
                for f in range(FC):
                    dve.wait_ge(h_in, e * FC + (f + 3))
                    dve.tensor_copy(hh[:, f, :], hidden[:, f % 2, :]).then_inc(h_high, 1)
                    dve.wait_ge(h_high, e * FC + (f + 1))
                    dve.tensor_tensor(hl[:, f, :], hidden[:, f % 2, :], hh[:, f, :].bitcast(F32),
                                      ALU.subtract).then_inc(h_parts, 1)
                if not last:
                    split_rows(e + 1, False)
                dve.wait_ge(s_ids, e + 1)
                for t in range(ST):
                    dve.wait_ge(y_ready, e * ST + (t + 2))
                    dve.tensor_tensor(ysum[:, t % 2, :], ps[:, 4 + t % 2, 0:D], b2[:, k, :], ALU.add).then_inc(y_sum, 1)
                    dve.wait_ge(y_sum, e * ST + (t + 3))
                    if t == 0:
                        dve.wait_ge(adds_done, e + 1)
                    dve.tensor_scalar(yout[:, t, :], ysum[:, t % 2, :], gain[:, k, t:t + 1], None,
                                      ALU.mult).then_inc(y_out, 1)

            experts(dve, expert)


_NAMES = {"x": "L0_attn_x", "Wq": "L0_attn_Wq", "bq": "L0_attn_bq", "Wk": "L0_attn_Wk", "bk": "L0_attn_bk",
          "Wv": "L0_attn_Wv", "bv": "L0_attn_bv", "Wo": "L0_attn_Wo", "bo": "L0_attn_bo", "Wr": "L0_ffn_Wr",
          "W1": "L0_ffn_W1", "b1": "L0_ffn_b1", "W2": "L0_ffn_W2", "b2": "L0_ffn_b2"}


def constants(np):
    freq = (np.float32(1.0) / np.float32(10000.0) ** (np.arange(0, DH, 2, dtype=np.float32) / np.float32(DH))).astype(np.float32)
    angle = (np.arange(S, dtype=np.float32)[None, :] * freq[:, None]).astype(np.float32)
    angle = np.tile(np.repeat(angle, 2, axis=0), (P // DH, 1))
    sign = np.where(np.arange(P) % 2 == 0, -1.0, 1.0).astype(np.float32)[:, None]
    bits = np.repeat((1 << np.arange(BITS - 1, -1, -1)).astype(np.int32)[:, None], E, axis=1)
    return {"c_ident": np.eye(P, dtype=np.float32), "c_cos": np.cos(angle).astype(np.float32),
            "c_sin": (np.sin(angle) * sign).astype(np.float32), "c_bits": bits}


def kernel(**inputs):
    import numpy as _np
    import concourse.bacc as _bacc
    from concourse import mybir as _mybir
    from concourse.bass_utils import run_bass_kernel_spmd as _run

    nc = _bacc.Bacc("TRN2", target_bir_lowering=False, num_devices=1)
    arrays, aps = {}, {}
    given = {short: _np.ascontiguousarray(inputs[name]) for short, name in _NAMES.items()}
    for name, chunks in (("bq", KC), ("bk", KC)):
        given[name] = _np.ascontiguousarray(given[name].reshape(chunks, P).T)
    given["b1"] = _np.ascontiguousarray(given["b1"].reshape(E, FC, P).transpose(0, 2, 1))
    for name, a in {**given, **constants(_np)}.items():
        arrays[f"in_{name}"] = a
        aps[name] = nc.dram_tensor(f"in_{name}", a.shape, _mybir.dt.from_np(a.dtype), kind="ExternalInput").ap()
    out = nc.dram_tensor("out_0", (B, S, D), _mybir.dt.float32, kind="ExternalOutput").ap()
    build(nc, aps, out)
    r = _run(nc, [arrays], core_ids=[0])
    return r.results[0]["out_0"]
```

```python
from contextlib import ExitStack

import concourse.bass as bass
from concourse import mybir

F32 = mybir.dt.float32
BF16 = mybir.dt.bfloat16
F32R = mybir.dt.float32r
I32 = mybir.dt.int32
U32 = mybir.dt.uint32
ALU = mybir.AluOpType
ACT = mybir.ActivationFunctionType
AX_X = mybir.AxisListType.X
RADD = bass.bass_isa.ReduceOp.add

P = 128
B, S, D = 4, 1024, 256
H, DH = 16, 16
E, DI = 8, 1024
TOK = B * S
TILES = TOK // P
CAP = 2 * TOK // E
KC = D // P
BLK = 512
NBLK = TOK // BLK
BT = BLK // P
HG = 4
GROUPS = B * H // HG
QT = S // P
HALF = S // 2
VW = 32
TERMS = ((0, 0), (0, 1), (1, 0), (0, 2), (2, 0), (1, 1))
SROWS = DH * len(TERMS)
MROWS = 3
ROW = D + E + 1
FIRST_BITS = 20
BITS = 30
FC = DI // P
ST = CAP // P
EPS = 1e-5
SCALE = float(D) ** -0.5
NOWHERE = 100000.0


def build(nc, a, out):
    with ExitStack() as top:
        xrow = nc.dram_tensor("xrow", (TOK, ROW), F32, kind="Internal").ap()
        slots_dram = nc.dram_tensor("slot_rows", (E * CAP, ROW), F32, kind="Internal").ap()
        qs_dram = nc.dram_tensor("q_parts", (3, GROUPS, 2 * HG, DH, HALF), BF16, kind="Internal").ap()
        ks_dram = nc.dram_tensor("k_parts", (3, GROUPS, 2 * HG, DH, HALF), BF16, kind="Internal").ap()
        v_dram = nc.dram_tensor("v_groups", (GROUPS, P, QT, HG * VW), F32, kind="Internal").ap()
        keep = Keep(nc, top)
        with ExitStack() as inner:
            stacks = Stacks(nc, inner, qs_dram, ks_dram, v_dram)
            with ExitStack() as ctx:
                norm_stage(nc, ctx, a, keep, stacks, xrow, qs_dram, ks_dram, v_dram)
            with ExitStack() as ctx:
                attention_stage(nc, ctx, keep, stacks, xrow, slots_dram)
        with ExitStack() as inner:
            given = ExpertLoads(nc, inner, a, slots_dram)
            with ExitStack() as ctx:
                project_stage(nc, ctx, a, keep, given, out)
            with ExitStack() as ctx:
                expert_stage(nc, ctx, keep, given, out)


class Keep:

    def __init__(self, nc, ctx):
        def sb(name, shape, dt):
            return ctx.enter_context(nc.sbuf_tensor(name, shape, dt))

        self.ident = sb("ident", [P, P], F32)
        self.identb = sb("identb", [P, P], BF16)
        self.slot = sb("slot", [P, TILES, E], U32)
        self.heads = sb("heads", [P, GROUPS // 2, QT, 2 * HG * DH], F32)
        self.upper = sb("upper", [P, P], BF16)
        self.ones = sb("ones", [P, P], BF16)
        self.tail = sb("tail", [P, TILES, E + 1], F32)
        self.prob = self.tail[:, :, 0:E]
        self.thr = sb("thr", [P, E], I32)
        self.bits_i = sb("bits_i", [P, BITS, E], I32)
        self.bits_f = sb("bits_f", [P, BITS, E], F32)
        self.tot = sb("tot", [P, E], F32)
        self.wo = sb("wo", [P, KC, D], F32)
        self.bo = sb("bo", [P, D], F32)
        self.psum = ctx.enter_context(nc.psum_tensor("psum", [P, 8, 512], F32))


class Stacks:

    def __init__(self, nc, ctx, qs_dram, ks_dram, v_dram):
        def sb(name, shape, dt=F32):
            return ctx.enter_context(nc.sbuf_tensor(name, shape, dt))

        self.qst = sb("qst", [P, 2, 2, HG, HALF], BF16)
        self.kst = sb("kst", [P, 2, 2, HG, HALF], BF16)
        self.vgr = sb("vgr", [P, 2, QT, HG * VW])
        self.landed = [ctx.enter_context(nc.semaphore("in_stack0")), ctx.enter_context(nc.semaphore("in_stack1"))]
        self.qs_dram, self.ks_dram, self.v_dram = qs_dram, ks_dram, v_dram

    LOADS = 2 * len(TERMS) + 1

    def load(self, sp, g, par, which=range(LOADS)):
        for n in which:
            r, of_k = n // 2, n % 2
            rows = slice(r * DH, (r + 1) * DH)
            if n == 2 * len(TERMS):
                sp.dma_start(self.vgr[:, par, :, :], self.v_dram[g]).then_inc(self.landed[par], 16)
            else:
                tile, dram = (self.kst, self.ks_dram) if of_k else (self.qst, self.qs_dram)
                sp.dma_start(tile[rows, par, :, :, :].rearrange("r h j s -> r (h j) s"),
                             dram[TERMS[r][of_k], g].rearrange("q r s -> r q s")).then_inc(self.landed[par], 16)


class ExpertLoads:
    NL = 3

    def __init__(self, nc, ctx, a, slots_dram):
        def sb(name, shape, dt=F32):
            return ctx.enter_context(nc.sbuf_tensor(name, shape, dt))

        def sem(name):
            return ctx.enter_context(nc.semaphore(name))

        self.w1 = sb("w1", [P, KC, DI])
        self.w2 = sb("w2", [P, FC, D])
        self.b1 = sb("b1", [P, 2, FC])
        self.b2 = sb("b2", [P, 2, D])
        self.rows = sb("rows", [P, 2, ST, ROW])
        self.in_w1 = sem("e_in_w1")
        self.in_w2 = sem("e_in_w2")
        self.in_rows = [sem("e_in_rows0"), sem("e_in_rows1")]
        self.b1_dram, self.b2_dram = a["b1"], a["b2"]
        self.slot_rows = slots_dram.rearrange("(e t p) c -> e p t c", e=E, p=P)
        self.w1_dram = a["W1"].rearrange("e (c p) n -> e p c n", p=P)
        self.w2_dram = a["W2"].rearrange("e (c p) n -> e p c n", p=P)

    def load_w1(self, sp, e):
        sp.dma_start(self.w1[:, :, :], self.w1_dram[e]).then_inc(self.in_w1, 16)

    def load_w2(self, sp, e):
        sp.dma_start(self.w2[:, :, :], self.w2_dram[e]).then_inc(self.in_w2, 16)

    def load_rows(self, sp, e, k):
        sp.dma_start(self.rows[:, k, :, :], self.slot_rows[e]).then_inc(self.in_rows[k], 16)
        sp.dma_start(self.b1[:, k, :], self.b1_dram[e]).then_inc(self.in_rows[k], 16)
        sp.dma_start(self.b2[:, k, :], self.b2_dram[e].partition_broadcast(P)).then_inc(self.in_rows[k], 16)


class Search:

    def __init__(self, ctx, nc, name):
        def sb(what, shape, dt=F32):
            return ctx.enter_context(nc.sbuf_tensor(name + what, shape, dt))

        self.cand = sb("cand", [P, E], I32)
        self.gain = sb("gain", [P, E], I32)
        self.diff = sb("diff", [P, TILES, E])
        self.tree = sb("tree", [P, TILES, E])
        self.took = sb("took", [P, E])
        self.s_step = ctx.enter_context(nc.semaphore(name + "step"))


def find_threshold(pool, keep, search, first_bit, end_bit):
    STEPS = 13
    cand, gain, diff, tree, took, s_step = search.cand, search.gain, search.diff, search.tree, search.took, search.s_step
    thr, tot = keep.thr, keep.tot
    with pool.Fori(first_bit, end_bit) as i:
        def chained(instruction, step):
            instruction.then_inc(s_step, 1)
            pool.wait_ge(s_step, step)

        bit_i = keep.bits_i[:, bass.ds(i, 1), :].rearrange("p o e -> p (o e)")
        bit_f = keep.bits_f[:, bass.ds(i, 1), :].rearrange("p o e -> p (o e)")
        chained(pool.tensor_tensor(cand[:, :], thr[:, :], bit_i, ALU.add), 1)
        chained(pool.tensor_tensor(diff[:, :, :], keep.prob[:, :, :],
                                   cand[:, :].bitcast(F32).unsqueeze(1).to_broadcast([P, TILES, E]),
                                   ALU.subtract), 2)
        chained(pool.tensor_scalar(tree[:, :, :], diff[:, :, :], 0.0, None, ALU.is_ge), 3)
        chained(pool.tensor_tensor(tree[:, 0:16, :], tree[:, 0:16, :], tree[:, 16:32, :], ALU.add), 4)
        chained(pool.tensor_tensor(tree[:, 0:8, :], tree[:, 0:8, :], tree[:, 8:16, :], ALU.add), 5)
        chained(pool.tensor_tensor(tree[:, 0:4, :], tree[:, 0:4, :], tree[:, 4:8, :], ALU.add), 6)
        chained(pool.tensor_tensor(tree[:, 0:2, :], tree[:, 0:2, :], tree[:, 2:4, :], ALU.add), 7)
        chained(pool.tensor_tensor(tree[:, 0, :], tree[:, 0, :], tree[:, 1, :], ALU.add), 8)
        chained(pool.partition_all_reduce(tot[:, :], tree[:, 0, :], P, RADD), 9)
        chained(pool.tensor_scalar(took[:, :], tot[:, :], float(CAP), None, ALU.is_ge), 10)
        chained(pool.tensor_tensor(took[:, :], took[:, :], bit_f, ALU.mult), 11)
        chained(pool.tensor_copy(gain[:, :], took[:, :]), 12)
        chained(pool.tensor_tensor(thr[:, :], thr[:, :], gain[:, :], ALU.add), 13)
        pool.sem_inc(s_step, -STEPS)


def norm_stage(nc, ctx, a, keep, stacks, xrow, qs_dram, ks_dram, v_dram):
    def sb(name, shape, dt=F32):
        return ctx.enter_context(nc.sbuf_tensor(name, shape, dt))

    def sem(name):
        return ctx.enter_context(nc.semaphore(name))

    ps = keep.psum
    xin = sb("xin", [P, 2, BT, D])
    xn = sb("xn", [P, 2, BT, D])
    stats = sb("stats", [P, 2, BT, 6])
    mean_var = sb("mean_var", [P, 2, BT, 2])
    var_eps = sb("var_eps", [P, 2, BT])
    std = sb("std", [P, 2, BT])
    rstd = sb("rstd", [P, 2, BT])
    xt = sb("xt", [P, 2, KC, BLK])
    xnt = sb("xnt", [P, KC, TOK])
    wvr = sb("wvr", [P, KC, D + E])
    wqk = sb("wqk", [P, 2, KC, D])
    bqk = sb("bqk", [P, 2, KC])
    bv = sb("bv", [P, D])
    vst = sb("vst", [P, 2, H // HG, BT, HG, VW])
    lg = sb("lg", [P, 2, BT, E])
    lmax = sb("lmax", [P, 2, BT])
    lsh = sb("lsh", [P, 2, BT, E])
    lexp = sb("lexp", [P, 2, BT, E])
    lsum = sb("lsum", [P, 2, BT])
    lrec = sb("lrec", [P, 2, BT])
    tid_i = sb("tid_i", [P, TILES], I32)
    cos = sb("cos", [P, S])
    sin = sb("sin", [P, S])
    qb = sb("qb", [P, 2, BLK])
    qsw = sb("qsw", [P, 2, BLK])
    qc = sb("qc", [P, 2, BLK])
    qsn = sb("qsn", [P, 2, BLK])
    qr = sb("qr", [P, 2, BLK])
    rest = sb("rest", [P, 2, BLK])
    parts = sb("parts", [P, 2, 3, BLK], BF16)
    upper, ones, thr = keep.upper, keep.ones, keep.thr
    bits_i, bits_f = keep.bits_i, keep.bits_f
    search = Search(ctx, nc, "early_")

    s_w = sem("s_w")
    s_bits = sem("s_bits")
    s_x = [sem("s_x0"), sem("s_x1")]
    s_stat = sem("s_stat")
    s_soft = sem("s_soft")
    s_var = sem("s_var")
    s_std = sem("s_std")
    s_xn = sem("s_xn")
    s_tr = sem("s_tr")
    s_xt = sem("s_xt")
    s_xnt = sem("s_xnt")
    s_vr = sem("s_vr")
    s_v = sem("s_v")
    s_sh = sem("s_sh")
    s_ex = sem("s_ex")
    s_prob = sem("s_prob")
    s_store = [sem("s_store0"), sem("s_store1")]
    s_vst = [sem("s_vst0"), sem("s_vst1")]
    s_tail = sem("s_tail")
    s_pool = sem("s_pool")
    s_const = sem("s_const")
    s_one = sem("s_one")
    s_pq = sem("s_pq")
    s_qb = sem("s_qb")
    s_rope = sem("s_rope")
    s_q1 = sem("s_q1")
    s_r1 = sem("s_r1")
    s_q2 = sem("s_q2")
    s_q3 = sem("s_q3")
    s_dve = sem("s_dve")
    s_qst = [sem("s_qst0"), sem("s_qst1")]
    NW = 6

    x_blocks = a["x"].rearrange("b (n t p) d -> (b n) p t d", p=P, t=BT)
    row_blocks = xrow[:, 0:D].rearrange("(n t p) c -> n p t c", p=P, t=BT)
    v_blocks = v_dram.rearrange("(b g) p (n t) c -> b n p g (t c)", g=H // HG, t=BT)
    q_blocks = [t.rearrange("a (b m g) (n j) r s -> b m n g (j r) a s", b=B, m=KC, n=S // BLK) for t in (qs_dram, ks_dram)]

    with nc.Block() as block:
        @block.sync
        def _(sp):
            def load_x(i, k):
                sp.dma_start(xin[:, k, :, :], x_blocks[i * 2 + k]).then_inc(s_x[k], 16)

            load_x(0, 0)
            for q, b in enumerate(("bq", "bk")):
                sp.dma_start(bqk[:, q, :], a[b]).then_inc(s_store[q], 16)
            sp.dma_start(keep.ident[:, :], a["c_ident"]).then_inc(s_w, 16)
            load_x(0, 1)
            for kc in range(KC):
                rows = slice(kc * P, (kc + 1) * P)
                sp.dma_start(wvr[:, kc, 0:D], a["Wv"][rows, :]).then_inc(s_w, 16)
                sp.dma_start(wvr[:, kc, D:D + E], a["Wr"][rows, :]).then_inc(s_w, 16)
            sp.dma_start(bv[:, :], a["bv"].partition_broadcast(P)).then_inc(s_w, 16)
            for q, w in enumerate(("Wq", "Wk")):
                sp.dma_start(wqk[:, q, :, :], a[w].rearrange("(c p) n -> p c n", p=P)).then_inc(s_vst[q], 16)
            sp.dma_start(cos[:, :], a["c_cos"]).then_inc(s_qst[0], 16)
            sp.dma_start(sin[:, :], a["c_sin"]).then_inc(s_qst[1], 16)

            def store_xn(i, k):
                sp.dma_start(row_blocks[i * 2 + k], xn[:, k, :, :]).then_inc(s_store[k], 16)

            def store_v(b, k):
                sp.wait_ge(s_v, b * 2 + (k + 2))
                sp.dma_start(v_blocks[b, k], vst[:, k, :, :, :, :].rearrange("p g t h w -> p g (t h w)")).then_inc(s_vst[k], 16)

            sp.wait_ge(s_xn, 1)
            store_xn(0, 0)
            load_x(1, 0)
            with sp.Fori(0, NBLK // 2 - 2) as i:
                for k in range(2):
                    sp.wait_ge(s_xn, i * 2 + (k + 2))
                    store_xn(i + k, 1 - k)
                    load_x(i + (1 + k), 1 - k)
                    store_v(i, k)
            for n in range(NBLK - 4, NBLK):
                if n + 1 < NBLK:
                    sp.wait_ge(s_xn, n + 2)
                    store_xn((n + 1) // 2, (n + 1) % 2)
                if n + 3 < NBLK:
                    load_x((n + 3) // 2, (n + 3) % 2)
                store_v(n // 2, n % 2)
            sp.wait_ge(s_const, 2)
            sp.wait_ge(s_prob, NBLK)
            sp.dma_start(xrow[:, D:ROW].rearrange("(t p) c -> p t c", p=P), keep.tail[:, :, :]).then_inc(s_tail, 16)

            def store_parts(b, last):
                for n in range(S // BLK):
                    for q in range(2):
                        for m in range(KC):
                            r = (n * 2 + q) * KC + m
                            k = r % 2
                            sp.wait_ge(s_q3, b * 8 + (r + 1))
                            for g in range(2):
                                sp.dma_start(q_blocks[q][b, m, n, g],
                                             parts[g * HG * DH:(g + 1) * HG * DH, k, :, :]).then_inc(s_qst[k], 16)
                            if last:
                                stacks.load(sp, 0, 0, range(2 * r, min(2 * r + 2, stacks.LOADS)))

            with sp.Fori(0, B - 1) as b:
                store_parts(b, False)
            for k in range(2):
                sp.wait_ge(s_vst[k], NBLK // 2 * 16 + 16)
                sp.wait_ge(s_qst[k], 4 * 2 * 16 + 16)
            store_parts(B - 1, True)
            sp.wait_ge(s_tail, 16)
            for k in range(2):
                sp.wait_ge(s_store[k], NBLK // 2 * 16 + 16)
                sp.wait_ge(s_qst[k], B * 4 * 2 * 16 + 16)

        @block.gpsimd
        def _(pool):
            pool.dma_start(bits_i[:, :, :], a["c_bits"].partition_broadcast(P)).then_inc(s_bits, 16)
            pool.memset(ones[:, :], 1.0).then_inc(s_pool, 1)
            pool.iota(tid_i[:, :], [[P, TILES]], 0, channel_multiplier=1).then_inc(s_pool, 1)
            pool.wait_ge(s_pool, 2)
            pool.affine_select(out=upper[:, :], in_=ones[:, :], compare_op=ALU.is_gt, fill=0.0, base=0,
                               pattern=[[1, P]], channel_multiplier=-1).then_inc(s_const, 1)
            pool.tensor_copy(keep.tail[:, :, E], tid_i[:, :]).then_inc(s_const, 1)
            pool.wait_ge(s_w, 16 * NW)
            pool.wait_ge(s_bits, 16)
            pool.tensor_copy(keep.identb[:, :], keep.ident[:, :]).then_inc(s_const, 1)
            pool.tensor_copy(bits_f[:, :, :], bits_i[:, :, :]).then_inc(s_const, 1)
            pool.memset(thr[:, :], 0).then_inc(s_const, 1)
            pool.wait_ge(s_const, 5)
            pool.memset(stacks.kst[SROWS:P, :, :, :, :], 1.0).then_inc(s_const, 1)
            pool.wait_ge(s_const, 6)
            pool.wait_ge(s_prob, NBLK)
            find_threshold(pool, keep, search, 0, FIRST_BITS)

        @block.vector
        def _(dve):
            dve.sem_inc(s_v, 1)

            def statistics(i, k):
                dve.wait_ge(s_x[k], i * 16 + 16)
                for t in range(BT):
                    dve.bn_stats(stats[:, k, t, :], xin[:, k, t, :]).then_inc(s_stat, 1)
                dve.wait_ge(s_stat, BT)
                for t in range(BT):
                    dve.bn_aggr(mean_var[:, k, t, :], stats[:, k, t, :]).then_inc(s_stat, 1)
                dve.wait_ge(s_stat, 2 * BT)
                dve.tensor_scalar(var_eps[:, k, :], mean_var[:, k, :, 1], EPS, None, ALU.add).then_inc(s_var, 1)

            def normalise(i, k, n):
                dve.wait_ge(s_std, n + 1)
                dve.reciprocal(rstd[:, k, :], std[:, k, :]).then_inc(s_stat, 1)
                dve.wait_ge(s_stat, 2 * BT + 1)
                dve.sem_inc(s_stat, -(2 * BT + 1))
                dve.wait_ge(s_store[k], i * 16 + 16)
                for t in range(BT):
                    last = dve.tensor_scalar(xn[:, k, t, :], xin[:, k, t, :], mean_var[:, k, t, 0:1],
                                             rstd[:, k, t:t + 1], ALU.subtract, ALU.mult)
                last.then_inc(s_xn, 1)

            def values(n, i, k):
                dve.wait_ge(s_vst[k], i * 16 + 16)
                for t in range(BT):
                    dve.wait_ge(s_vr, n * BT + (t + 1))
                    dve.tensor_tensor(vst[:, k, :, t, :, 0:DH], ps[:, 4 + t, 0:D].rearrange("p (g h d) -> p g h d", g=H // HG, d=DH),
                                      bv[:, :].rearrange("p (g h d) -> p g h d", g=H // HG, d=DH), ALU.add)
                dve.tensor_copy(lg[:, k, :, :], ps[:, 4:4 + BT, D:D + E]).then_inc(s_v, 1)
                dve.wait_ge(s_v, n + 2)
                dve.tensor_reduce(lmax[:, k, :], lg[:, k, :, :], AX_X, ALU.max).then_inc(s_soft, 1)
                dve.wait_ge(s_soft, 1)
                dve.tensor_tensor(lsh[:, k, :, :], lg[:, k, :, :],
                                  lmax[:, k, :].unsqueeze(2).to_broadcast([P, BT, E]), ALU.subtract).then_inc(s_sh, 1)

            def probabilities(n, k):
                dve.wait_ge(s_ex, n + 1)
                dve.tensor_reduce(lsum[:, k, :], lexp[:, k, :, :], AX_X, ALU.add).then_inc(s_soft, 1)
                dve.wait_ge(s_soft, 2)
                dve.reciprocal(lrec[:, k, :], lsum[:, k, :]).then_inc(s_soft, 1)
                dve.wait_ge(s_soft, 3)
                dve.sem_inc(s_soft, -3)
                dve.tensor_tensor(keep.tail[:, bass.ds(n * BT, BT), 0:E], lexp[:, k, :, :],
                                  lrec[:, k, :].unsqueeze(2).to_broadcast([P, BT, E]), ALU.mult).then_inc(s_prob, 1)

            def blocks(i, last):
                for k in range(2):
                    n = i * 2 + k
                    if not (last and k == 1):
                        normalise(i + k, 1 - k, n + 1)
                    values(n, i, k)
                    if not last:
                        statistics(i + 1, k)
                    probabilities(n, k)

            statistics(0, 0)
            normalise(0, 0, 0)
            statistics(0, 1)
            dve.memset(vst[:, :, :, :, :, :], 1.0).then_inc(s_one, 1)
            dve.wait_ge(s_one, 1)
            dve.wait_ge(s_w, 16 * NW)
            with dve.Fori(0, NBLK // 2 - 1) as i:
                blocks(i, False)
            blocks(NBLK // 2 - 1, True)

            swap = [j ^ 1 for j in range(32)]
            for k in range(2):
                dve.wait_ge(s_qst[k], 16)

            def turn(n, r):
                k = r % 2
                pos = slice(BLK * (r // 4), BLK * (r // 4) + BLK)
                dve.wait_ge(s_qb, n + 3)
                dve.tensor_tensor(qc[:, k, :], qb[:, k, :], cos[:, pos], ALU.mult).then_inc(s_dve, 1)
                dve.stream_shuffle(qsw[:, k, :], qb[:, k, :], swap).then_inc(s_dve, 1)

            def rotate(n, r):
                k = r % 2
                pos = slice(BLK * (r // 4), BLK * (r // 4) + BLK)
                dve.wait_ge(s_dve, n * 3 + 2)
                dve.tensor_tensor(qsn[:, k, :], qsw[:, k, :], sin[:, pos], ALU.mult).then_inc(s_dve, 1)
                dve.wait_ge(s_dve, n * 3 + 3)
                dve.tensor_tensor(qr[:, k, :], qc[:, k, :], qsn[:, k, :], ALU.add).then_inc(s_rope, 1)

            def products(b, last):
                for r in range(8):
                    k = r % 2
                    n = b * 8 + r
                    more = not (last and r == 7)
                    if more:
                        turn(n + 1, (r + 1) % 8)
                    dve.wait_ge(s_q1, n + 1)
                    dve.tensor_tensor(rest[:, k, :], qr[:, k, :], parts[:, k, 0, :], ALU.subtract).then_inc(s_r1, 1)
                    if more:
                        rotate(n + 1, (r + 1) % 8)
                    dve.wait_ge(s_q2, n + 1)
                    dve.tensor_tensor(parts[:, k, 2, :], rest[:, k, :], parts[:, k, 1, :], ALU.subtract).then_inc(s_q3, 1)

            turn(0, 0)
            rotate(0, 0)
            with dve.Fori(0, B - 1) as b:
                products(b, False)
            products(B - 1, True)

        @block.scalar
        def _(act):
            act.sem_inc(s_xnt, 1)
            act.sem_inc(s_qb, 2)
            def turned(n, k):
                act.wait_ge(s_tr, n * 2 + 1)
                act.copy(xt[:, k, 0, :], ps[:, k * 2, :]).then_inc(s_xt, 1)
                act.wait_ge(s_tr, n * 2 + 2)
                act.copy(xt[:, k, 1, :], ps[:, k * 2 + 1, :]).then_inc(s_xt, 1)

            def kept(n, k):
                for kc in range(KC):
                    act.copy(xnt[:, kc, bass.ds(n * BLK, BLK)], ps[:, k * 2 + kc, :]).then_inc(s_xnt, 1)

            def blocks(i, last):
                for k in range(2):
                    n = i * 2 + k
                    if not (last and k == 1):
                        turned(n + 1, 1 - k)
                    act.wait_ge(s_sh, n + 1)
                    act.activation(lexp[:, k, :, :], lsh[:, k, :, :], ACT.Exp).then_inc(s_ex, 1)
                    if not last:
                        act.wait_ge(s_var, n + 3)
                        act.activation(std[:, k, :], var_eps[:, k, :], ACT.Sqrt).then_inc(s_std, 1)
                    if not (last and k == 1):
                        kept(n + 1, 1 - k)

            for k in range(2):
                act.wait_ge(s_var, k + 1)
                act.activation(std[:, k, :], var_eps[:, k, :], ACT.Sqrt).then_inc(s_std, 1)
            act.wait_ge(s_tr, 1)
            act.copy(xt[:, 0, 0, :], ps[:, 0, :]).then_inc(s_xt, 1)
            act.wait_ge(s_tr, 2)
            act.copy(xt[:, 0, 1, :], ps[:, 1, :]).then_inc(s_xt, 1)
            for kc in range(KC):
                act.copy(xnt[:, kc, 0:BLK], ps[:, kc, :]).then_inc(s_xnt, 1)
            with act.Fori(0, NBLK // 2 - 1) as i:
                blocks(i, False)
            blocks(NBLK // 2 - 1, True)
            for q in range(2):
                act.wait_ge(s_store[q], 16)

            def biased(n, r):
                k, q, m = r % 2, r // 2 % 2, r % 2
                act.wait_ge(s_pq, n + 1)
                act.activation(qb[:, k, :], ps[:, k, :], ACT.Identity, bias=bqk[:, q, m:m + 1]).then_inc(s_qb, 1)

            def products(b, last):
                for r in range(8):
                    k = r % 2
                    n = b * 8 + r
                    act.wait_ge(s_rope, n + 1)
                    act.wait_ge(s_qst[k], b * 128 + (32 * (r // 2) + 16))
                    act.copy(parts[:, k, 0, :], qr[:, k, :]).then_inc(s_q1, 1)
                    if not (last and r >= 6):
                        biased(n + 2, (r + 2) % 8)
                    act.wait_ge(s_r1, n + 1)
                    act.copy(parts[:, k, 1, :], rest[:, k, :]).then_inc(s_q2, 1)

            for r in range(2):
                biased(r, r)
            with act.Fori(0, B - 1) as b:
                products(b, False)
            products(B - 1, True)

        @block.tensor
        def _(pe):
            pe.wait_ge(s_w, 16 * NW)
            def turn(n, k):
                for kc in range(KC):
                    for t in range(BT):
                        last = pe.transpose(ps[:, k * 2 + kc, t * P:(t + 1) * P],
                                            xn[:, k, t, kc * P:(kc + 1) * P], keep.ident[:, :])
                    last.then_inc(s_tr, 1)

            def blocks(i, last):
                for k in range(2):
                    n = i * 2 + k
                    pe.wait_ge(s_xt, n * 2 + 2)
                    pe.wait_ge(s_v, n + 1)
                    for t in range(BT):
                        for kc in range(KC):
                            done = pe.matmul(ps[:, 4 + t, 0:D + E], xt[:, k, kc, t * P:(t + 1) * P],
                                             wvr[:, kc, :], start=(kc == 0), stop=(kc == KC - 1))
                        done.then_inc(s_vr, 1)
                    if not (last and k == 1):
                        pe.wait_ge(s_xn, n + 2)
                        pe.wait_ge(s_xnt, n * KC + 1)
                        turn(n + 1, 1 - k)

            pe.wait_ge(s_xn, 1)
            turn(0, 0)
            with pe.Fori(0, NBLK // 2 - 1) as i:
                blocks(i, False)
            blocks(NBLK // 2 - 1, True)
            with pe.Fori(0, B) as b:
                pe.wait_ge(s_xnt, KC * NBLK + 1)
                for q in range(2):
                    pe.wait_ge(s_vst[q], 16)
                for r in range(8):
                    k, blk, q, m = r % 2, r // 4, r // 2 % 2, r % 2
                    pe.wait_ge(s_qb, b * 8 + (r + 1))
                    for kc in range(KC):
                        last = pe.matmul(ps[:, k, :], wqk[:, q, kc, m * P:(m + 1) * P],
                                         xnt[:, kc, bass.ds(b * S + blk * BLK, BLK)],
                                         start=(kc == 0), stop=(kc == KC - 1))
                    last.then_inc(s_pq, 1)


def attention_stage(nc, ctx, keep, stacks, xrow, slots_dram):
    def sb(name, shape, dt=F32):
        return ctx.enter_context(nc.sbuf_tensor(name, shape, dt))

    def sem(name):
        return ctx.enter_context(nc.semaphore(name))

    ps = keep.psum
    SB, TB, OB = 0, 4, 6
    qst, kst, vgr, in_stack = stacks.qst, stacks.kst, stacks.vgr, stacks.landed
    pt = sb("pt", [P, 2, HG, HALF])
    mx = sb("mx", [P, 2, HG, QT // 2])
    negm = sb("negm", [P, 2, 2 * MROWS, HG, QT // 2], BF16)
    mrest = sb("mrest", [P, 2, HG, QT // 2])
    mrow = sb("mrow", [MROWS * HG * QT // 2, 2, P], BF16)
    osb = sb("osb", [P, 2, HALF])
    den = sb("den", [P, 2, QT // 2, HG])
    stage = sb("stage", [P, 2, ROW])
    where = sb("where", [P, 2, E], U32)

    prob, thr, tot = keep.prob, keep.thr, keep.tot
    diff = sb("a_diff", [P, TILES, E])
    mask = sb("mask", [P, 2, TILES, E], BF16)
    inside = sb("inside", [P, 2, TILES, E])
    off0 = sb("off0", [P, 2, TILES, E])
    off1 = sb("off1", [P, 2, TILES, E])
    rank = sb("rank", [P, 2, TILES, E])
    fits = sb("fits", [P, TILES, E])
    slot_f = sb("slot_f", [P, TILES, E])
    slot_t = sb("slot_t", [P, TILES, E])

    search = Search(ctx, nc, "late_")

    s_slot = sem("s_slot")
    s_mask = sem("s_mask")
    s_pre = sem("s_pre")
    s_ins = sem("s_ins")
    s_const = sem("a_const")
    st_ready = sem("st_ready")
    exp_done = sem("exp_done")
    pv_done = sem("pv_done")
    s_ready = sem("s_ready")
    max_done = sem("max_done")
    split = sem("split")
    neg_ready = sem("neg_ready")
    neg_t = sem("neg_t")
    mrow_ready = sem("mrow_ready")
    mrow_in = [sem("mrow_in0"), sem("mrow_in1")]
    o_copied = sem("o_copied")
    o_t = sem("o_t")
    o_rec = sem("o_rec")
    o_norm = sem("o_norm")
    in_row = [sem("in_row0"), sem("in_row1")]
    s_freed = sem("s_freed")
    s_where = sem("s_where")
    sent = [sem("sent0"), sem("sent1")]
    UNITS = 2 * QT
    LAG = 4
    NLOAD = stacks.LOADS
    FIRST_TILES = QT * HG // 2
    LATE = FIRST_TILES // LAG
    TURN_A, TURN_B = 12, 4

    with nc.Block() as block:
        @block.sync
        def _(sp):
            def put_max(g, par, half):
                sp.wait_ge(mrow_ready, g * 2 + (half + 1))
                n = HG * QT // 2
                for part in range(MROWS):
                    sp.dma_start(qst[SROWS + part:SROWS + part + 1, par, half, :, :].rearrange("o j (q t) -> o (j q) t", t=P),
                                 mrow[part * n:(part + 1) * n, half, :]).then_inc(mrow_in[half], 16)

            stacks.load(sp, 1, 1)
            put_max(0, 0, 0)
            put_max(0, 0, 1)

            def group(g, par):
                put_max(g + 1, 1 - par, 0)
                sp.wait_ge(pv_done, g * UNITS + UNITS)
                stacks.load(sp, g + 2, par)
                put_max(g + 1, 1 - par, 1)

            with sp.Fori(0, (GROUPS - 2) // 2) as i:
                for par in range(2):
                    group(i * 2 + par, par)
            put_max(GROUPS - 1, 1, 0)
            put_max(GROUPS - 1, 1, 1)

        @block.gpsimd
        def _(pool):
            rows = xrow.rearrange("(t p) c -> t p c", p=P)

            def load(t, par):
                pool.dma_start(stage[:, par, :], rows[t]).then_inc(in_row[par], 16)

            load(0, 0)
            load(1, 1)
            done = [0]

            def chain(instruction):
                done[0] += 1
                instruction.then_inc(s_slot, 1)
                pool.wait_ge(s_slot, done[0])

            find_threshold(pool, keep, search, FIRST_BITS, BITS)
            chain(pool.tensor_tensor(diff[:, :, :], prob[:, :, :],
                                     thr[:, :].bitcast(F32).unsqueeze(1).to_broadcast([P, TILES, E]), ALU.subtract))
            pool.tensor_scalar(mask[:, 0, :, :], diff[:, :, :], 0.0, None, ALU.is_gt).then_inc(s_mask, 1)
            pool.tensor_scalar(mask[:, 1, :, :], diff[:, :, :], 0.0, None, ALU.is_equal).then_inc(s_mask, 1)
            pool.wait_ge(s_ins, 4)
            src, dst = off0, off1
            for shift in (1, 2, 4, 8, 16):
                chain(pool.tensor_copy(dst[:, :, 0:shift, :], src[:, :, 0:shift, :]))
                chain(pool.tensor_tensor(dst[:, :, shift:TILES, :], src[:, :, shift:TILES, :],
                                         src[:, :, 0:TILES - shift, :], ALU.add))
                src, dst = dst, src
            chain(pool.tensor_tensor(rank[:, :, :, :], src[:, :, :, :], inside[:, :, :, :], ALU.add))
            above = dst
            chain(pool.tensor_tensor(above[:, 0, 0, :], rank[:, 0, TILES - 1, :], mask[:, 0, TILES - 1, :], ALU.add))
            chain(pool.affine_select(out=above[:, 0, 1, :], in_=above[:, 0, 0, :], compare_op=ALU.is_ge, fill=0.0,
                                     base=-(P - 1), pattern=[[0, E]], channel_multiplier=1))
            chain(pool.partition_all_reduce(tot[:, :], above[:, 0, 1, :], P, RADD))
            chain(pool.tensor_tensor(rank[:, 1, :, :], rank[:, 1, :, :],
                                     tot[:, :].unsqueeze(1).to_broadcast([P, TILES, E]), ALU.add))
            chain(pool.tensor_scalar(fits[:, :, :], rank[:, 1, :, :], float(CAP), None, ALU.is_lt))
            chain(pool.tensor_tensor(fits[:, :, :], fits[:, :, :], mask[:, 1, :, :], ALU.mult))
            for e in range(E):
                chain(pool.tensor_scalar(rank[:, :, :, e], rank[:, :, :, e], float(CAP * e) - NOWHERE, None, ALU.add))
            chain(pool.tensor_tensor(slot_f[:, :, :], rank[:, 0, :, :], mask[:, 0, :, :], ALU.mult))
            chain(pool.tensor_tensor(slot_t[:, :, :], rank[:, 1, :, :], fits[:, :, :], ALU.mult))
            chain(pool.tensor_tensor(slot_f[:, :, :], slot_f[:, :, :], slot_t[:, :, :], ALU.add))
            chain(pool.tensor_scalar(keep.slot[:, :, :], slot_f[:, :, :], NOWHERE, None, ALU.add))

            def scatter(i, par):
                pool.tensor_copy(where[:, par, :], keep.slot[:, bass.ds(i * 2 + par, 1), :].rearrange("p o e -> p (o e)"))\
                    .then_inc(s_where, 1)
                pool.wait_ge(s_where, 1)
                pool.wait_ge(in_row[par], i * 16 + 16)
                pool.sem_inc(s_where, -1)
                for e in range(E):
                    pool.indirect_dma_start(
                        out=slots_dram[:, :], out_offset=bass.IndirectOffsetOnAxis(ap=where[:, par, e:e + 1], axis=0),
                        in_=stage[:, par, :], in_offset=None, bounds_check=E * CAP - 1, oob_is_err=False,
                    ).then_inc(sent[par], 16)

            with pool.Fori(0, TILES // 2 - 1) as i:
                for par in range(2):
                    scatter(i, par)
                for par in range(2):
                    pool.wait_ge(sent[par], i * (16 * E) + 16 * E)
                    pool.sem_inc(s_freed, 1)
                    load(i * 2 + (par + 2), par)
            for par in range(2):
                scatter(TILES // 2 - 1, par)
            for par in range(2):
                pool.wait_ge(sent[par], TILES // 2 * E * 16)

        @block.tensor
        def _(pe):
            def scores_t(g, par, u, half_turn):
                half, kt = u // QT, u % QT
                for j in range(HG):
                    n = g * (UNITS * HG) + (u * HG + j)
                    if j == 0 and u % QT == 0:
                        pe.wait_ge(mrow_in[half], g * (16 * MROWS) + 16 * MROWS)
                    if not (isinstance(g, int) and n < 2):
                        pe.wait_ge(exp_done, n - 1)
                    pe.matmul(ps[:, TB + j % 2, :], kst[0:SROWS + MROWS, par, kt // 4, j, kt % 4 * P:(kt % 4 + 1) * P],
                              qst[0:SROWS + MROWS, par, half, j, :],
                              start=True, stop=True).then_inc(st_ready, 1)
                    yield

            def scores(g, par, s):
                qt, j = s // HG, s % HG
                n = g * (QT * HG) + s
                if not (isinstance(g, int) and n < 2):
                    pe.wait_ge(max_done, n - 1)
                for half in range(2):
                    last = pe.matmul(ps[:, SB + 2 * (s % 2) + half, :], qst[0:SROWS, par, qt // 4, j, qt % 4 * P:(qt % 4 + 1) * P],
                                     kst[0:SROWS, par, half, j, :], start=True, stop=True)
                last.then_inc(s_ready, 1)

            def outputs(g, par, u):
                half, kt = u // QT, u % QT
                if kt == 0:
                    pe.wait_ge(mrow_ready, g * 2 + (half + 1))
                pe.wait_ge(exp_done, g * (UNITS * HG) + (u + 1) * HG)
                for j in range(HG):
                    last = pe.matmul(ps[VW * j:VW * (j + 1), OB + half, :], vgr[:, par, kt, VW * j:VW * (j + 1)],
                                     pt[:, u % 2, j, :], start=(kt == 0), stop=(kt == QT - 1))
                last.then_inc(pv_done, 1)

            def turn_max(g, half):
                n = MROWS * HG * QT // 2
                pe.wait_ge(neg_ready, g * 2 + (half + 1))
                pe.transpose(ps[0:2 * n, OB + half, 0:P // 2].bitcast(BF16),
                             negm[:, half, :, :, :].rearrange("p a j q -> p (a j q)"), keep.identb[:, :]).then_inc(neg_t, 1)

            def turn_outputs(g, half):
                pe.wait_ge(o_copied, g * 2 + (half + 1))
                for t in range(QT // 2):
                    last = pe.transpose(ps[:, OB + half, t * P:(t + 1) * P], osb[:, half, t * P:(t + 1) * P],
                                        keep.ident[:, :])
                last.then_inc(o_t, 1)

            def count(weights):
                flat_mask = mask[:, :, :, :].rearrange("p m t e -> p (m t e)")
                pe.matmul(ps[:, OB, :], weights[:, :], flat_mask, start=True, stop=True).then_inc(s_pre, 1)

            pe.wait_ge(in_stack[0], 16 * NLOAD)
            for s in range(FIRST_TILES):
                scores(0, 0, s)
            turn_max(0, 0)
            for _ in scores_t(0, 0, 0, 0):
                pass

            def tiles_of_scores(g, par, u, first, last):
                if u >= LAG and not last:
                    return [(g + 1, 1 - par, 2 * (u - LAG) + n) for n in range(2)]
                if u < LAG and not first:
                    return [(g, par, 2 * (u + UNITS - LAG) + n) for n in range(2)]
                if u < LAG and first:
                    return [(g, par, FIRST_TILES + LATE * u + n) for n in range(LATE)]
                return []

            def group(g, par, turns, first, last):
                for u in range(UNITS):
                    tiles = tiles_of_scores(g, par, u, first, last)
                    if u == LAG and not last:
                        pe.wait_ge(in_stack[1 - par], turns * (16 * NLOAD) + 16 * NLOAD)
                    if u + 1 < UNITS:
                        ahead = scores_t(g, par, u + 1, 0)
                    else:
                        ahead = scores_t(g + 1, 1 - par, 0, 0) if not last else iter(())
                    next(ahead, None)
                    for tile in tiles:
                        scores(*tile)
                    next(ahead, None)
                    next(ahead, None)
                    outputs(g, par, u)
                    for _ in ahead:
                        pass
                    if u == 2 and not first:
                        turn_outputs(g - 1, 1)
                    if u == TURN_B:
                        if not first:
                            pe.wait_ge(o_norm, g * 2)
                        turn_max(g, 1)
                    if u == QT + 2:
                        turn_outputs(g, 0)
                    if u == TURN_A and not last:
                        pe.wait_ge(o_norm, g * 2 + 1)
                        turn_max(g + 1, 0)
                    if first and u == UNITS - 2:
                        pe.wait_ge(mrow_ready, 3)
                        pe.wait_ge(s_mask, 2)
                        count(keep.upper)
                    if first and u == UNITS - 1:
                        pe.wait_ge(s_ins, 2)
                        count(keep.ones)

            group(0, 0, 0, True, False)
            pe.wait_ge(s_ins, 4)
            with pe.Fori(0, (GROUPS - 2) // 2) as i:
                group(i * 2 + 1, 1, i + 1, False, False)
                group(i * 2 + 2, 0, i + 1, False, False)
            group(GROUPS - 1, 1, None, False, True)
            turn_outputs(GROUPS - 1, 1)

        @block.scalar
        def _(act):
            def rows_of_max(g, half):
                n = MROWS * HG * QT // 2
                act.wait_ge(neg_t, g * 2 + (half + 1))
                if not (isinstance(g, int) and g == 0):
                    act.wait_ge(mrow_in[half], g * (16 * MROWS))
                act.copy(mrow[:, half, :], ps[0:n, OB + half, 0:P // 2].bitcast(BF16)).then_inc(mrow_ready, 1)

            def copy_outputs(g, half):
                act.wait_ge(pv_done, g * UNITS + (half + 1) * QT)
                if not (isinstance(g, int) and g == 0):
                    act.wait_ge(o_t, g * 2 + (half - 1))
                act.copy(osb[:, half, :], ps[:, OB + half, :]).then_inc(o_copied, 1)

            def group(g, first, last):
                for u in range(UNITS):
                    if not (first and u < 2):
                        act.wait_ge(pv_done, g * UNITS + (u - 1))
                    for j in range(HG):
                        act.wait_ge(st_ready, g * (UNITS * HG) + (u * HG + j + 1))
                        act.activation(pt[:, u % 2, j, :], ps[:, TB + j % 2, :], ACT.Exp, scale=SCALE).then_inc(exp_done, 1)
                    if u == 1 and not first:
                        copy_outputs(g - 1, 1)
                    if u == TURN_B + 1:
                        rows_of_max(g, 1)
                    if u == QT + 1:
                        copy_outputs(g, 0)
                    if u == TURN_A + 1 and not last:
                        rows_of_max(g + 1, 0)

            rows_of_max(0, 0)
            group(0, True, False)
            with act.Fori(0, GROUPS - 2) as i:
                group(i + 1, False, False)
            group(GROUPS - 1, False, True)
            copy_outputs(GROUPS - 1, 1)

        @block.vector
        def _(dve):
            dve.memset(negm[:, :, :, :, :], 0.0).then_inc(s_const, 1)
            dve.memset(off0[:, :, 0, :], 0.0).then_inc(s_ins, 1)
            dve.wait_ge(s_const, 1)

            def take_max(g, s):
                qt, j = s // HG, s % HG
                dve.wait_ge(s_ready, g * (QT * HG) + (s + 1))
                dve.tensor_reduce(mx[:, qt // 4, j, qt % 4:qt % 4 + 1], ps[:, SB + 2 * (s % 2):SB + 2 * (s % 2) + 2, :]
                                  .rearrange("p b n -> p (b n)"), AX_X, ALU.max).then_inc(max_done, 1)

            def split_max(g, half):
                m = mx[:, half, :, :]
                dve.wait_ge(max_done, g * (QT * HG) + (half + 1) * (QT * HG // 2))
                if not (isinstance(g, int) and g == 0):
                    dve.wait_ge(neg_t, g * 2 + (half - 1))
                at = g * 6 + 3 * half
                dve.tensor_scalar(negm[:, half, 0, :, :], m, -1.0, None, ALU.mult).then_inc(split, 1)
                dve.wait_ge(split, at + 1)
                dve.scalar_tensor_tensor(out=mrest[:, half, :, :], in0=m, scalar=-1.0, in1=negm[:, half, 0, :, :],
                                         op0=ALU.mult, op1=ALU.subtract).then_inc(split, 1)
                dve.wait_ge(split, at + 2)
                dve.tensor_copy(negm[:, half, 1, :, :], mrest[:, half, :, :]).then_inc(split, 1)
                dve.wait_ge(split, at + 3)
                dve.tensor_tensor(negm[:, half, 2, :, :], mrest[:, half, :, :], negm[:, half, 1, :, :],
                                  ALU.subtract).then_inc(neg_ready, 1)

            def normalise(pair, par, half):
                g = pair * 2 + par
                o = ps[:, OB + half, :].rearrange("p (t j w) -> p t j w", t=QT // 2, j=HG)
                dve.wait_ge(o_t, g * 2 + (half + 1))
                dve.reciprocal(den[:, half, :, :], o[:, :, :, DH]).then_inc(o_rec, 1)
                dve.wait_ge(o_rec, g * 2 + (half + 1))
                where_to = keep.heads[:, bass.ds(pair, 1), half * (QT // 2):(half + 1) * (QT // 2),
                                      par * HG * DH:(par + 1) * HG * DH]
                dve.tensor_tensor(where_to.rearrange("p o t (j d) -> p (o t) j d", j=HG), o[:, :, :, 0:DH],
                                  den[:, half, :, :].unsqueeze(3).to_broadcast([P, QT // 2, HG, DH]),
                                  ALU.mult).then_inc(o_norm, 1)

            for s in range(FIRST_TILES):
                take_max(0, s)
            split_max(0, 0)

            def group(pair, par, first, last):
                g = pair * 2 + par
                for u in range(UNITS):
                    for n in range(2):
                        if u >= LAG and not last:
                            take_max(g + 1, 2 * (u - LAG) + n)
                        if u < LAG and not first:
                            take_max(g, 2 * (u + UNITS - LAG) + n)
                    if u < LAG and first:
                        for n in range(LATE):
                            take_max(g, FIRST_TILES + LATE * u + n)
                    if u == LAG + QT - 1 and not last:
                        split_max(g + 1, 0)
                    if u == LAG - 1:
                        split_max(g, 1)
                    if u == 2 and not first:
                        normalise(pair - (1 - par), 1 - par, 1)
                    if u == QT + 2:
                        normalise(pair, par, 0)
                    if first and u == UNITS - 1:
                        counts = ps[:, OB, :].rearrange("p (m t e) -> p m t e", m=2, t=TILES)
                        dve.wait_ge(s_pre, 1)
                        dve.tensor_copy(inside[:, :, :, :], counts).then_inc(s_ins, 1)
                        dve.wait_ge(s_pre, 2)
                        for m in range(2):
                            dve.tensor_copy(off0[:, m, 1:TILES, :], counts[:, m, 0:TILES - 1, :]).then_inc(s_ins, 1)

            group(0, 0, True, False)
            with dve.Fori(0, (GROUPS - 2) // 2) as i:
                group(i, 1, False, False)
                group(i + 1, 0, False, False)
            group(GROUPS // 2 - 1, 1, False, True)
            normalise(GROUPS // 2 - 1, 1, 1)


def project_stage(nc, ctx, a, keep, given, out):
    def sb(name, shape, dt=F32):
        return ctx.enter_context(nc.sbuf_tensor(name, shape, dt))

    def sem(name):
        return ctx.enter_context(nc.semaphore(name))

    ps = keep.psum
    PB = 4
    xres = sb("xres", [P, 2, PB, D])
    base = sb("base", [P, 2, PB, D])
    fin = sb("fin", [P, 2, PB, D])
    turn = sb("turn", [P, 2, KC, P])
    ht = sb("ht", [P, 2, KC, P])
    in_x = [sem("p_x0"), sem("p_x1")]
    s_turn = sem("p_turn")
    s_ht = sem("p_turned")
    s_hc = sem("p_copied")
    s_y = sem("p_product")
    s_base = sem("p_base")
    s_fin = sem("p_final")
    s_seen = sem("p_seen")
    stored = [sem("p_stored0"), sem("p_stored1")]
    x_blocks = a["x"].rearrange("b (h t p) d -> (b h) p t d", p=P, t=PB)
    out_blocks = out.rearrange("b (h t p) d -> (b h) p t d", p=P, t=PB)

    with nc.Block() as block:
        @block.sync
        def _(sp):
            sp.dma_start(keep.wo[:, :, :], a["Wo"].rearrange("(c p) n -> p c n", p=P)).then_inc(stored[0], 16)
            sp.dma_start(keep.bo[:, :], a["bo"].partition_broadcast(P)).then_inc(stored[1], 16)
            for h in range(2):
                sp.dma_start(xres[:, h, :, :], x_blocks[h]).then_inc(in_x[h], 16)
            given.load_w1(sp, 0)

            def store(b, h):
                sp.wait_ge(s_fin, b * QT + (PB * (h + 1) + 2))
                sp.dma_start(out_blocks[b * 2 + h], fin[:, h, :, :]).then_inc(stored[h], 16)

            with sp.Fori(0, B - 1) as b:
                for h in range(2):
                    store(b, h)
                    sp.dma_start(xres[:, h, :, :], x_blocks[b * 2 + (h + 2)]).then_inc(in_x[h], 16)
            given.load_rows(sp, 0, 0)
            given.load_w2(sp, 0)
            given.load_rows(sp, 1, 1)
            for h in range(2):
                store(B - 1, h)
            for h in range(2):
                sp.wait_ge(stored[h], B * 16 + 16)

        @block.gpsimd
        def _(pool):
            with pool.Fori(0, B) as b:
                for q in range(QT):
                    pool.wait_ge(s_ht, b * QT + (q + 1))
                    pool.sem_inc(s_seen, 1)
                    pool.tensor_copy(turn[:, q % 2, :, :],
                                     keep.heads[:, bass.ds(b * KC, KC), q, :]).then_inc(s_turn, 1)

        @block.tensor
        def _(pe):
            def turn_tile(b, q):
                pe.wait_ge(s_turn, b * QT + (q + 1))
                pe.wait_ge(s_hc, b * QT + (q + 1))
                for kc in range(KC):
                    last = pe.transpose(ps[:, q % 2, kc * P:(kc + 1) * P], turn[:, q % 2, kc, :], keep.ident[:, :])
                last.then_inc(s_ht, 1)

            def product(b, q):
                k = q % 2
                pe.wait_ge(s_hc, b * QT + (q + 3))
                pe.wait_ge(s_fin, b * QT + (q + 1))
                for kc in range(KC):
                    last = pe.matmul(ps[:, 2 + k, 0:D], ht[:, k, kc, :], keep.wo[:, kc, :],
                                     start=(kc == 0), stop=(kc == KC - 1))
                last.then_inc(s_y, 1)

            pe.sem_inc(s_ht, 2)
            pe.sem_inc(s_y, 2)
            pe.wait_ge(stored[0], 16)
            turn_tile(0, 0)
            with pe.Fori(0, B - 1) as b:
                for q in range(QT):
                    turn_tile(b, q + 1)
                    product(b, q)
            for q in range(QT):
                if q < QT - 1:
                    turn_tile(B - 1, q + 1)
                product(B - 1, q)

        @block.scalar
        def _(act):
            act.sem_inc(s_hc, 2)
            with act.Fori(0, B) as b:
                for q in range(QT):
                    k = q % 2
                    act.wait_ge(s_ht, b * QT + (q + 3))
                    act.wait_ge(s_y, b * QT + (q + 1))
                    act.copy(ht[:, k, :, :].rearrange("p c n -> p (c n)"), ps[:, k, 0:KC * P]).then_inc(s_hc, 1)

        @block.vector
        def _(dve):
            dve.sem_inc(s_fin, 2)
            dve.wait_ge(stored[1], 16)
            with dve.Fori(0, B) as b:
                for h in range(2):
                    dve.wait_ge(in_x[h], b * 16 + 16)
                    dve.tensor_tensor(base[:, h, :, :], xres[:, h, :, :],
                                      keep.bo[:, :].unsqueeze(1).to_broadcast([P, PB, D]), ALU.add).then_inc(s_base, 1)
                    dve.wait_ge(s_base, b * 2 + (h + 1))
                    dve.wait_ge(stored[h], b * 16 + 16)
                    for t in range(PB):
                        q = h * PB + t
                        dve.wait_ge(s_y, b * QT + (q + 3))
                        dve.tensor_tensor(fin[:, h, t, :], ps[:, 2 + q % 2, 0:D], base[:, h, t, :], ALU.add).then_inc(s_fin, 1)


def expert_stage(nc, ctx, keep, given, out):
    def sb(name, shape, dt=F32):
        return ctx.enter_context(nc.sbuf_tensor(name, shape, dt))

    def sem(name):
        return ctx.enter_context(nc.semaphore(name))

    ps = keep.psum
    w1, w2, b1, b2, rows = given.w1, given.w2, given.b1, given.b2, given.rows
    in_w1, in_w2, in_rows, NL = given.in_w1, given.in_w2, given.in_rows, given.NL
    w1h = sb("w1_high", [P, KC, DI], F32R)
    w1l = sb("w1_low", [P, KC, DI], F32R)
    w2h = sb("w2_high", [P, FC, D], F32R)
    w2l = sb("w2_low", [P, FC, D], F32R)
    xh = sb("x_high", [P, KC, CAP], F32R)
    xl = sb("x_low", [P, KC, CAP], F32R)
    hidden = sb("hidden", [P, 2, CAP])
    hh = sb("h_high", [P, FC, CAP], F32R)
    hl = sb("h_low", [P, FC, CAP], F32R)
    ids = sb("ids", [P, 2, ST], U32)
    gain = sb("e_gain", [P, 2, ST])
    ysum = sb("ysum", [P, 2, D])
    yout = sb("yout", [P, ST, D])
    w1h_ready = sem("e_w1_high")
    w1l_ready = sem("e_w1_low")
    w2h_ready = sem("e_w2_high")
    w2l_ready = sem("e_w2_low")
    turned = sem("e_turned")
    x_high = sem("e_x_high")
    x_in = sem("e_x_in")
    h_ready = sem("e_h_ready")
    h_in = sem("e_h_in")
    h_high = sem("e_h_high")
    h_parts = sem("e_h_parts")
    y_ready = sem("e_y_ready")
    y_sum = sem("e_y_sum")
    y_out = sem("e_y_out")
    s_ids = sem("e_ids")
    s_seen = sem("e_seen")
    added = sem("e_added")
    adds_done = sem("e_adds_done")
    TURN = (6, 7, 0, 1)
    OUT = (4, 5, 2, 3)
    out_rows = out.rearrange("b s d -> (b s) d")

    with nc.Block() as block:
        def experts(engine, expert):
            with engine.Fori(0, E // 2 - 1) as i:
                for k in range(2):
                    expert(i * 2 + k, k, False)
            for k in range(2):
                expert(E - 2 + k, k, k == 1)

        @block.sync
        def _(sp):
            def weights(e):
                sp.wait_ge(w1l_ready, e)
                given.load_w1(sp, e)
                sp.wait_ge(w2l_ready, e)
                given.load_w2(sp, e)

            with sp.Fori(0, E // 2 - 1) as i:
                for k in range(2):
                    weights(i * 2 + (k + 1))
                    sp.wait_ge(y_out, i * (2 * ST) + (k + 1) * ST)
                    given.load_rows(sp, i * 2 + (k + 2), k)
            weights(E - 1)

        @block.gpsimd
        def _(pool):
            def low(part, whole, high, ready):
                pool.tensor_tensor(part, whole, high.bitcast(F32), ALU.subtract).then_inc(ready, 1)

            pool.sem_inc(adds_done, 1)
            pool.wait_ge(w1h_ready, 1)
            low(w1l[:, :, :], w1[:, :, :], w1h[:, :, :], w1l_ready)

            def expert(e, k, last):
                pool.wait_ge(w2h_ready, e + 1)
                low(w2l[:, :, :], w2[:, :, :], w2h[:, :, :], w2l_ready)
                if not last:
                    pool.wait_ge(w1h_ready, e + 2)
                    low(w1l[:, :, :], w1[:, :, :], w1h[:, :, :], w1l_ready)
                pool.wait_ge(s_ids, e + 1)
                pool.sem_inc(s_seen, 1)
                for t in range(ST):
                    pool.wait_ge(y_out, e * ST + (t + 1))
                    pool.sem_inc(s_seen, 1)
                    pool.indirect_dma_start(
                        out=out_rows, out_offset=bass.IndirectOffsetOnAxis(ap=ids[:, k, t:t + 1], axis=0),
                        in_=yout[:, t, :], in_offset=None, bounds_check=TOK - 1, compute_op=ALU.add,
                    ).then_inc(added, 16)
                pool.wait_ge(added, e * (16 * ST) + 16 * ST)
                pool.sem_inc(adds_done, 1)

            experts(pool, expert)

        @block.tensor
        def _(pe):
            def turn_rows(e, k, first):
                pe.wait_ge(in_rows[k], 16 * NL if first else (e - k) * (8 * NL) + 16 * NL)
                for b in range(4):
                    kc, half = b // 2, b % 2
                    if b < 2 and not first:
                        pe.wait_ge(x_in, e * 4 + (b - 1))
                    elif b == 2 and not first:
                        pe.wait_ge(h_in, e * FC + 1)
                    for t in range(4):
                        last = pe.transpose(ps[:, TURN[b], t * P:(t + 1) * P],
                                            rows[:, k, half * 4 + t, kc * P:(kc + 1) * P], keep.ident[:, :])
                    last.then_inc(turned, 1)

            pe.sem_inc(y_ready, 1)
            turn_rows(0, 0, True)

            def expert(e, k, last):
                pe.wait_ge(w1l_ready, e + 1)
                pe.wait_ge(x_in, e * 4 + 4)
                for f in range(FC):
                    pe.wait_ge(h_in, e * FC + (f + 1))
                    if f == 1:
                        pe.wait_ge(y_sum, e * ST + 4)
                    chunk = slice(f * P, (f + 1) * P)
                    parts = [(w, x, kc) for w, x in ((w1h, xh), (w1h, xl), (w1l, xh)) for kc in range(KC)]
                    for n, (w, x, kc) in enumerate(parts):
                        for half in range(2):
                            done = pe.matmul(ps[:, 2 * (f % 2) + half, :], w[:, kc, chunk],
                                             x[:, kc, half * 512:(half + 1) * 512],
                                             start=(n == 0), stop=(n == len(parts) - 1))
                    done.then_inc(h_ready, 1)
                if not last:
                    turn_rows(e + 1, 1 - k, False)
                pe.wait_ge(w2l_ready, e + 1)

                def outputs(t, chunks):
                    slots = slice(t * P, (t + 1) * P)
                    for f in chunks:
                        if t == 0:
                            pe.wait_ge(h_parts, e * FC + (f + 3))
                        for n, (h, w) in enumerate(((hh, w2h), (hh, w2l), (hl, w2h))):
                            done = pe.matmul(ps[:, OUT[t % 4], 0:D], h[:, f, slots], w[:, f, :],
                                             start=(f == 0 and n == 0), stop=(f == FC - 1 and n == 2))
                    if FC - 1 in chunks:
                        done.then_inc(y_ready, 1)

                for chunks in (range(FC - 1), range(FC - 1, FC)):
                    for t in range(2):
                        if 0 in chunks:
                            pe.wait_ge(y_sum, e * ST + (t + 1))
                        outputs(t, chunks)
                for t in range(2, ST):
                    pe.wait_ge(y_sum, e * ST + (t + 1))
                    outputs(t, range(FC))

            experts(pe, expert)

        @block.scalar
        def _(act):
            act.sem_inc(h_in, 2)
            act.wait_ge(in_w1, 16)
            act.copy(w1h[:, :, :], w1[:, :, :]).then_inc(w1h_ready, 1)

            def expert(e, k, last):
                act.wait_ge(y_ready, e * ST + 1)
                act.wait_ge(in_w2, e * 16 + 16)
                act.copy(w2h[:, :, :], w2[:, :, :]).then_inc(w2h_ready, 1)
                for f in range(FC):
                    act.wait_ge(h_ready, e * FC + (f + 1))
                    act.wait_ge(h_parts, e * FC + (f + 1))
                    act.activation(hidden[:, f % 2, :].rearrange("p (b n) -> p b n", b=2),
                                   ps[:, 2 * (f % 2):2 * (f % 2) + 2, :],
                                   ACT.Gelu, bias=b1[:, k, f:f + 1]).then_inc(h_in, 1)
                if not last:
                    act.wait_ge(in_w1, e * 16 + 32)
                    act.copy(w1h[:, :, :], w1[:, :, :]).then_inc(w1h_ready, 1)

            experts(act, expert)

        @block.vector
        def _(dve):
            def split_rows(e, first):
                for b in range(4):
                    kc, half = b // 2, b % 2
                    at = slice(half * 512, (half + 1) * 512)
                    dve.wait_ge(turned, b + 1 if first else e * 4 + (b + 1))
                    dve.tensor_copy(xh[:, kc, at], ps[:, TURN[b], :]).then_inc(x_high, 1)
                    dve.wait_ge(x_high, b + 1 if first else e * 4 + (b + 1))
                    dve.tensor_tensor(xl[:, kc, at], ps[:, TURN[b], :], xh[:, kc, at].bitcast(F32),
                                      ALU.subtract).then_inc(x_in, 1)

            dve.sem_inc(y_sum, 4)
            dve.sem_inc(h_parts, 2)
            split_rows(0, True)

            def expert(e, k, last):
                dve.wait_ge(in_rows[k], (e - k) * (8 * NL) + 16 * NL)
                dve.tensor_copy(gain[:, k, :], rows[:, k, :, bass.ds(e + D, 1)].rearrange("p t o -> p (t o)"))
                dve.tensor_copy(ids[:, k, :], rows[:, k, :, ROW - 1]).then_inc(s_ids, 1)
                for f in range(FC):
                    dve.wait_ge(h_in, e * FC + (f + 3))
                    dve.tensor_copy(hh[:, f, :], hidden[:, f % 2, :]).then_inc(h_high, 1)
                    dve.wait_ge(h_high, e * FC + (f + 1))
                    dve.tensor_tensor(hl[:, f, :], hidden[:, f % 2, :], hh[:, f, :].bitcast(F32),
                                      ALU.subtract).then_inc(h_parts, 1)
                if not last:
                    split_rows(e + 1, False)
                dve.wait_ge(s_ids, e + 1)
                for t in range(ST):
                    dve.wait_ge(y_ready, e * ST + (t + 2))
                    dve.tensor_tensor(ysum[:, t % 2, :], ps[:, OUT[t % 4], 0:D], b2[:, k, :], ALU.add).then_inc(y_sum, 1)
                    dve.wait_ge(y_sum, e * ST + (t + 5))
                    if t == 0:
                        dve.wait_ge(adds_done, e + 1)
                    dve.tensor_scalar(yout[:, t, :], ysum[:, t % 2, :], gain[:, k, t:t + 1], None,
                                      ALU.mult).then_inc(y_out, 1)

            experts(dve, expert)


_NAMES = {"x": "L0_attn_x", "Wq": "L0_attn_Wq", "bq": "L0_attn_bq", "Wk": "L0_attn_Wk", "bk": "L0_attn_bk",
          "Wv": "L0_attn_Wv", "bv": "L0_attn_bv", "Wo": "L0_attn_Wo", "bo": "L0_attn_bo", "Wr": "L0_ffn_Wr",
          "W1": "L0_ffn_W1", "b1": "L0_ffn_b1", "W2": "L0_ffn_W2", "b2": "L0_ffn_b2"}


def constants(np):
    freq = (np.float32(1.0) / np.float32(10000.0) ** (np.arange(0, DH, 2, dtype=np.float32) / np.float32(DH))).astype(np.float32)
    angle = (np.arange(S, dtype=np.float32)[None, :] * freq[:, None]).astype(np.float32)
    angle = np.tile(np.repeat(angle, 2, axis=0), (P // DH, 1))
    sign = np.where(np.arange(P) % 2 == 0, -1.0, 1.0).astype(np.float32)[:, None]
    bits = np.repeat((1 << np.arange(BITS - 1, -1, -1)).astype(np.int32)[:, None], E, axis=1)
    return {"c_ident": np.eye(P, dtype=np.float32), "c_cos": np.cos(angle).astype(np.float32),
            "c_sin": (np.sin(angle) * sign).astype(np.float32), "c_bits": bits}


def kernel(**inputs):
    import numpy as _np
    import concourse.bacc as _bacc
    from concourse import mybir as _mybir
    from concourse.bass_utils import run_bass_kernel_spmd as _run

    nc = _bacc.Bacc("TRN2", target_bir_lowering=False, num_devices=1)
    arrays, aps = {}, {}
    given = {short: _np.ascontiguousarray(inputs[name]) for short, name in _NAMES.items()}
    for name, chunks in (("bq", KC), ("bk", KC)):
        given[name] = _np.ascontiguousarray(given[name].reshape(chunks, P).T)
    given["b1"] = _np.ascontiguousarray(given["b1"].reshape(E, FC, P).transpose(0, 2, 1))
    for name, a in {**given, **constants(_np)}.items():
        arrays[f"in_{name}"] = a
        aps[name] = nc.dram_tensor(f"in_{name}", a.shape, _mybir.dt.from_np(a.dtype), kind="ExternalInput").ap()
    out = nc.dram_tensor("out_0", (B, S, D), _mybir.dt.float32, kind="ExternalOutput").ap()
    build(nc, aps, out)
    r = _run(nc, [arrays], core_ids=[0])
    return r.results[0]["out_0"]
```
